# Optimizing a Trainium2 kernel written in Bass

```python
import numpy as np
import jax
import jax.numpy as jnp

def _softmax(x, axis=-1):
    return jax.nn.softmax(x, axis=axis)

def _gelu(x):
    return jax.nn.gelu(x, approximate=True)

def _silu(x):
    return jax.nn.silu(x)

def _sigmoid(x):
    return jax.nn.sigmoid(x)

def _layernorm(x, axis=-1, eps=1e-05):
    m = jnp.mean(x, axis=axis, keepdims=True)
    v = jnp.var(x, axis=axis, keepdims=True)
    return (x - m) / jnp.sqrt(v + eps)

def _scatter_add(tgt, idx, src, axis=0):
    return tgt.at[idx].add(src)

def _segment_sum(src, seg, n):
    return jax.ops.segment_sum(src, seg, n)
kernel_name = 'mk_decoder_postln_d1_seqx_r8_bf8306'

def setup_inputs(seed: int=0):
    np.random.seed(seed)
    _w = jnp.asarray

    def _rec_inputs():
        import jax
        import jax.numpy as jnp
        _rk = jax.random.key(seed)
        x = -0.000125 + 0.9999 * jax.random.normal(jax.random.fold_in(_rk, 1), (16, 128, 256), jnp.float32)
        _lenS = 128 - jax.random.randint(jax.random.fold_in(_rk, 7), (16,), 0, max(1, 128 // 4) + 1, jnp.int32)
        _lenS2 = 128 - jax.random.randint(jax.random.fold_in(_rk, 8), (16,), 0, max(1, 128 // 4) + 1, jnp.int32)
        _ctx_2048P = jax.random.normal(jax.random.fold_in(_rk, 11), (16, 16, 256), jnp.float32)
        _ctx_2048c = jax.random.dirichlet(jax.random.fold_in(_rk, 511), 0.3 * jnp.ones((16,), jnp.float32), (16, 128))
        _ctx_2048t = jnp.einsum('bsk,bkd->bsd', _ctx_2048c, _ctx_2048P)
        _ctx_2048t = _ctx_2048t * jax.lax.rsqrt(jnp.mean(jnp.square(_ctx_2048t)) + 1e-12) * 0.953939
        ctx_2048 = -0.000514642 + 1.00011 * (_ctx_2048t + 0.3 * jax.random.normal(jax.random.fold_in(_rk, 611), (16, 128, 256), jnp.float32))
        _validS = jnp.arange(128)[None, :] < _lenS[:, None]
        _validS2 = jnp.arange(128)[None, :] < _lenS2[:, None]
        _causal = jnp.tril(jnp.ones((128, 128), dtype=bool))
        mask_BxS2_bk0 = jnp.logical_not(jnp.broadcast_to(_validS2[:, :], (16, 128)))
        return (x, ctx_2048, mask_BxS2_bk0)
    x, ctx_2048, mask_BxS2_bk0 = _rec_inputs()

    def _L0_attn_setup():
        import jax, jax.numpy as jnp
        import numpy as np
        D_MODEL = 256
        N_HEADS = 16
        D_HEAD = D_MODEL // N_HEADS
        B, S = (2, 256)
        EPS = 1e-05

        def _mhsa(X, ln_g, ln_b, Wq, bq, Wk, bk, Wv, bv, Wo, bo):
            n_ctx = X.shape[-2]
            mu = jnp.mean(X, axis=-1, keepdims=True)
            var = jnp.mean(jnp.square(X - mu), axis=-1, keepdims=True)
            Xn = (X - mu) * jax.lax.rsqrt(var + EPS) * ln_g + ln_b

            def split_heads(t):
                return t.reshape(t.shape[:-1] + (N_HEADS, D_HEAD)).swapaxes(-2, -3)
            Q = split_heads(Xn @ Wq + bq)
            K = split_heads(Xn @ Wk + bk)
            V = split_heads(Xn @ Wv + bv)
            scores = jnp.einsum('bhqd,bhkd->bhqk', Q, K) / jnp.sqrt(jnp.float32(D_HEAD))
            causal = jnp.tril(jnp.ones((n_ctx, n_ctx), dtype=bool))
            scores = jnp.where(causal, scores, jnp.float32(-jnp.inf))
            A = jax.nn.softmax(scores, axis=-1)
            AV = jnp.einsum('bhqk,bhkd->bhqd', A, V)
            AV = AV.swapaxes(-2, -3).reshape(X.shape[:-1] + (D_MODEL,))
            return AV @ Wo + bo
        key = jax.random.key(seed)
        ks = jax.random.split(key, 10)
        sd = 1.0 / np.sqrt(D_MODEL)
        inp = {'X': jax.random.normal(ks[0], (B, S, D_MODEL), dtype=jnp.float32), 'ln_g': jnp.ones((D_MODEL,), jnp.float32), 'ln_b': jnp.zeros((D_MODEL,), jnp.float32), 'Wq': jax.random.uniform(ks[1], (D_MODEL, D_MODEL), jnp.float32, -sd, sd), 'bq': jax.random.uniform(ks[2], (D_MODEL,), jnp.float32, -sd, sd), 'Wk': jax.random.uniform(ks[3], (D_MODEL, D_MODEL), jnp.float32, -sd, sd), 'bk': jax.random.uniform(ks[4], (D_MODEL,), jnp.float32, -sd, sd), 'Wv': jax.random.uniform(ks[5], (D_MODEL, D_MODEL), jnp.float32, -sd, sd), 'bv': jax.random.uniform(ks[6], (D_MODEL,), jnp.float32, -sd, sd), 'Wo': jax.random.uniform(ks[7], (D_MODEL, D_MODEL), jnp.float32, -sd, sd), 'bo': jax.random.uniform(ks[8], (D_MODEL,), jnp.float32, -sd, sd)}
        return inp
    _L0_attn_all = _L0_attn_setup()
    _L0_attn_in = {k: v for k, v in _L0_attn_all.items() if k in ('ln_g', 'ln_b', 'Wq', 'bq', 'Wk', 'bk', 'Wv', 'bv', 'Wo', 'bo')}
    del _L0_attn_all

    def _L0_xattn_setup():
        import jax, jax.numpy as jnp
        import numpy as np
        H = 256
        NH = 16
        HD = H // NH
        EPS = 1e-06

        def rmsnorm(x, w, eps=EPS):
            var = jnp.mean(x * x, axis=-1, keepdims=True)
            return x * jax.lax.rsqrt(var + eps) * w
        key = jax.random.key(seed)
        ks = jax.random.split(key, 9)
        B, L, M = (4, 512, 32)
        s = 1.0 / np.sqrt(H)
        return {'hidden_states': jax.random.normal(ks[0], (B, L, H), dtype=jnp.float32), 'memory_tokens': jax.random.normal(ks[1], (B, M, H), dtype=jnp.float32), 'memory_mask': jax.random.randint(ks[2], (B, M), 0, 2).astype(bool), 'norm_w': jnp.ones((H,), dtype=jnp.float32), 'wq': jax.random.normal(ks[3], (H, H), dtype=jnp.float32) * s, 'wk': jax.random.normal(ks[4], (H, H), dtype=jnp.float32) * s, 'wv': jax.random.normal(ks[5], (H, H), dtype=jnp.float32) * s, 'wo': jax.random.normal(ks[6], (H, H), dtype=jnp.float32) * s, 'wg': jax.random.normal(ks[7], (H, H), dtype=jnp.float32) * s}
    _L0_xattn_all = _L0_xattn_setup()
    _L0_xattn_in = {k: v for k, v in _L0_xattn_all.items() if k in ('norm_w', 'wq', 'wk', 'wv', 'wo', 'wg')}
    del _L0_xattn_all

    def _L0_ffn_setup():
        import jax, jax.numpy as jnp
        import numpy as np
        NUM_EXPERTS = 8
        TOP_K = 2
        IN_DIM = 256
        BOT_DIM = 64
        BATCH, SEQ = (4, 256)

        def _gelu(x):
            return jax.nn.gelu(x, approximate=False)
        key = jax.random.key(seed)
        ks = jax.random.split(key, 8)
        scale_d = 1.0 / np.sqrt(IN_DIM)
        scale_b = 1.0 / np.sqrt(BOT_DIM)
        return {'hidden_states': jax.random.normal(ks[0], (BATCH, SEQ, IN_DIM), jnp.float32), 'gate_w': jax.random.normal(ks[1], (NUM_EXPERTS, IN_DIM), jnp.float32) * scale_d, 'wd': jax.random.normal(ks[2], (NUM_EXPERTS, BOT_DIM, IN_DIM), jnp.float32) * scale_d, 'bd': jnp.zeros((NUM_EXPERTS, BOT_DIM), jnp.float32), 'wu': jax.random.normal(ks[3], (NUM_EXPERTS, IN_DIM, BOT_DIM), jnp.float32) * scale_b * 0.02, 'bu': jnp.zeros((NUM_EXPERTS, IN_DIM), jnp.float32), 'ws_d': jax.random.normal(ks[4], (BOT_DIM, IN_DIM), jnp.float32) * scale_d, 'bs_d': jnp.zeros((BOT_DIM,), jnp.float32), 'ws_u': jax.random.normal(ks[5], (IN_DIM, BOT_DIM), jnp.float32) * scale_b * 0.02, 'bs_u': jnp.zeros((IN_DIM,), jnp.float32)}
    _L0_ffn_all = _L0_ffn_setup()
    _L0_ffn_in = {k: v for k, v in _L0_ffn_all.items() if k in ('gate_w', 'wd', 'bd', 'wu', 'bu', 'ws_d', 'bs_d', 'ws_u', 'bs_u')}
    del _L0_ffn_all
    return {'x': x, 'ctx_2048': ctx_2048, 'mask_BxS2_bk0': mask_BxS2_bk0, 'L0_attn_ln_g': _L0_attn_in['ln_g'], 'L0_attn_ln_b': _L0_attn_in['ln_b'], 'L0_attn_Wq': _L0_attn_in['Wq'], 'L0_attn_bq': _L0_attn_in['bq'], 'L0_attn_Wk': _L0_attn_in['Wk'], 'L0_attn_bk': _L0_attn_in['bk'], 'L0_attn_Wv': _L0_attn_in['Wv'], 'L0_attn_bv': _L0_attn_in['bv'], 'L0_attn_Wo': _L0_attn_in['Wo'], 'L0_attn_bo': _L0_attn_in['bo'], 'L0_xattn_norm_w': _L0_xattn_in['norm_w'], 'L0_xattn_wq': _L0_xattn_in['wq'], 'L0_xattn_wk': _L0_xattn_in['wk'], 'L0_xattn_wv': _L0_xattn_in['wv'], 'L0_xattn_wo': _L0_xattn_in['wo'], 'L0_xattn_wg': _L0_xattn_in['wg'], 'L0_ffn_gate_w': _L0_ffn_in['gate_w'], 'L0_ffn_wd': _L0_ffn_in['wd'], 'L0_ffn_bd': _L0_ffn_in['bd'], 'L0_ffn_wu': _L0_ffn_in['wu'], 'L0_ffn_bu': _L0_ffn_in['bu'], 'L0_ffn_ws_d': _L0_ffn_in['ws_d'], 'L0_ffn_bs_d': _L0_ffn_in['bs_d'], 'L0_ffn_ws_u': _L0_ffn_in['ws_u'], 'L0_ffn_bs_u': _L0_ffn_in['bs_u']}

def reference(x, ctx_2048, mask_BxS2_bk0, L0_attn_ln_g, L0_attn_ln_b, L0_attn_Wq, L0_attn_bq, L0_attn_Wk, L0_attn_bk, L0_attn_Wv, L0_attn_bv, L0_attn_Wo, L0_attn_bo, L0_xattn_norm_w, L0_xattn_wq, L0_xattn_wk, L0_xattn_wv, L0_xattn_wo, L0_xattn_wg, L0_ffn_gate_w, L0_ffn_wd, L0_ffn_bd, L0_ffn_wu, L0_ffn_bu, L0_ffn_ws_d, L0_ffn_bs_d, L0_ffn_ws_u, L0_ffn_bs_u):
    import jax
    import jax.numpy as jnp

    def _L0_attn_ref(X, ln_g, ln_b, Wq, bq, Wk, bk, Wv, bv, Wo, bo):
        import jax, jax.numpy as jnp
        import numpy as np
        D_MODEL = 256
        N_HEADS = 16
        D_HEAD = D_MODEL // N_HEADS
        B, S = (2, 256)
        EPS = 1e-05

        def _mhsa(X, ln_g, ln_b, Wq, bq, Wk, bk, Wv, bv, Wo, bo):
            n_ctx = X.shape[-2]
            mu = jnp.mean(X, axis=-1, keepdims=True)
            var = jnp.mean(jnp.square(X - mu), axis=-1, keepdims=True)
            Xn = (X - mu) * jax.lax.rsqrt(var + EPS) * ln_g + ln_b

            def split_heads(t):
                return t.reshape(t.shape[:-1] + (N_HEADS, D_HEAD)).swapaxes(-2, -3)
            Q = split_heads(Xn @ Wq + bq)
            K = split_heads(Xn @ Wk + bk)
            V = split_heads(Xn @ Wv + bv)
            scores = jnp.einsum('bhqd,bhkd->bhqk', Q, K) / jnp.sqrt(jnp.float32(D_HEAD))
            causal = jnp.tril(jnp.ones((n_ctx, n_ctx), dtype=bool))
            scores = jnp.where(causal, scores, jnp.float32(-jnp.inf))
            A = jax.nn.softmax(scores, axis=-1)
            AV = jnp.einsum('bhqk,bhkd->bhqd', A, V)
            AV = AV.swapaxes(-2, -3).reshape(X.shape[:-1] + (D_MODEL,))
            return AV @ Wo + bo
        return _mhsa(X, ln_g, ln_b, Wq, bq, Wk, bk, Wv, bv, Wo, bo)

    def _L0_xattn_ref(hidden_states, memory_tokens, memory_mask, norm_w, wq, wk, wv, wo, wg):
        import jax, jax.numpy as jnp
        import numpy as np
        H = 256
        NH = 16
        HD = H // NH
        EPS = 1e-06

        def rmsnorm(x, w, eps=EPS):
            var = jnp.mean(x * x, axis=-1, keepdims=True)
            return x * jax.lax.rsqrt(var + eps) * w
        B, L, C = hidden_states.shape
        M = memory_tokens.shape[1]
        scale = HD ** (-0.5)
        x = rmsnorm(hidden_states, norm_w)
        q = (x @ wq.T).reshape(B, L, NH, HD)
        k = (memory_tokens @ wk.T).reshape(B, M, NH, HD)
        v = (memory_tokens @ wv.T).reshape(B, M, NH, HD)
        attn = jnp.einsum('blhd,bmhd->bhlm', q, k) * scale
        attn = jnp.where(memory_mask[:, None, None, :], attn, -jnp.inf)
        attn = jax.nn.softmax(attn, axis=-1)
        attn = jnp.nan_to_num(attn, nan=0.0)
        out = jnp.einsum('bhlm,bmhd->blhd', attn, v).reshape(B, L, C)
        out = out @ wo.T
        gate = jax.nn.sigmoid(x @ wg.T)
        return gate * out

    def _L0_ffn_ref(hidden_states, gate_w, wd, bd, wu, bu, ws_d, bs_d, ws_u, bs_u):
        import jax, jax.numpy as jnp
        import numpy as np
        NUM_EXPERTS = 8
        TOP_K = 2
        IN_DIM = 256
        BOT_DIM = 64
        BATCH, SEQ = (4, 256)

        def _gelu(x):
            return jax.nn.gelu(x, approximate=False)
        B, S, D = hidden_states.shape
        x = hidden_states.reshape(-1, D)
        T = x.shape[0]
        logits = x @ gate_w.T
        probs = jax.nn.softmax(logits.astype(jnp.float32), axis=-1)
        rw, sel = jax.lax.top_k(probs, TOP_K)
        rw = rw / rw.sum(axis=-1, keepdims=True)
        rw = rw.astype(x.dtype)
        combine = jnp.zeros((T, NUM_EXPERTS), x.dtype).at[jnp.arange(T)[:, None], sel].add(rw)
        down = jnp.einsum('td,ebd->teb', x, wd) + bd[None]
        h = _gelu(down) * combine[:, :, None]
        expert_out = jnp.einsum('teb,edb->td', h, wu) + combine @ bu
        shared = _gelu(x @ ws_d.T + bs_d) @ ws_u.T + bs_u
        out = (expert_out + shared).reshape(B, S, D)
        return out
    x = _layernorm(x + _L0_attn_ref(x, L0_attn_ln_g, L0_attn_ln_b, L0_attn_Wq, L0_attn_bq, L0_attn_Wk, L0_attn_bk, L0_attn_Wv, L0_attn_bv, L0_attn_Wo, L0_attn_bo), axis=-1)
    x = _layernorm(x + _L0_xattn_ref(x, ctx_2048, mask_BxS2_bk0, L0_xattn_norm_w, L0_xattn_wq, L0_xattn_wk, L0_xattn_wv, L0_xattn_wo, L0_xattn_wg), axis=-1)
    x = _layernorm(x + _L0_ffn_ref(x, L0_ffn_gate_w, L0_ffn_wd, L0_ffn_bd, L0_ffn_wu, L0_ffn_bu, L0_ffn_ws_d, L0_ffn_bs_d, L0_ffn_ws_u, L0_ffn_bs_u), axis=-1)
    return x

_drawn_inputs = setup_inputs


def setup_inputs(seed=0):
    import zlib

    import numpy as np

    out = dict(_drawn_inputs(seed))
    spreads = {'L0_attn_ln_g': (1.0, 0.6),
     'L0_attn_ln_b': (0.0, 0.1),
     'L0_xattn_norm_w': (1.0, 0.2),
     'L0_ffn_bd': (0.0, 0.8),
     'L0_ffn_bu': (0.0, 0.1),
     'L0_ffn_bs_d': (0.0, 0.8),
     'L0_ffn_bs_u': (0.0, 0.1)}
    factors = {'L0_attn_bq': 8.0,
     'L0_attn_bk': 8.0,
     'L0_ffn_wd': 6.542,
     'L0_ffn_wu': 5.862,
     'L0_ffn_ws_d': 4.81,
     'L0_ffn_ws_u': 4.34}
    for name, (base, spread) in spreads.items():
        noise = np.random.default_rng([zlib.crc32(name.encode()), seed]).standard_normal(out[name].shape)
        drawn = base * np.exp(spread * noise) if base else spread * noise
        out[name] = jnp.asarray(drawn.astype(out[name].dtype))
    for name, factor in factors.items():
        out[name] = (out[name] * factor).astype(out[name].dtype)
    return out
```

```python
import concourse.bass as bass
from concourse import mybir
from contextlib import ExitStack

F32 = mybir.dt.float32
BF16 = mybir.dt.bfloat16
U8 = mybir.dt.uint8
ALU = mybir.AluOpType
ACT = mybir.ActivationFunctionType
AX = mybir.AxisListType

NB = 16
P = 128
D = 256
KC = D // P
NH = 16
DH = D // NH
NR = 4
NE = 8
BD = 64
EC = NE * BD // P
SCALE = DH ** -0.5
BIG = -1.0e30
EPS_LN = 1e-5
EPS_RMS = 1e-6
WEIGHTS = 11


def decoder_layer(nc, x, ctx_in, mask, cols_in, rows_in, wa_in, wo_a_in, wb_in, wdn_in, wup_in, wsu_in,
                  bu_in, bsd_in, out):
    es = ExitStack()
    with es:
        def sb(name, shape, dt=F32):
            return es.enter_context(nc.sbuf_tensor(name, shape, dt))

        def sem(name):
            return es.enter_context(nc.semaphore(name))

        identf = sb("identf", [P, P])
        identb = sb("identb", [P, P], BF16)
        ones = sb("ones", [P, P])
        onesb = sb("onesb", [P, P], BF16)
        neg_half, eps_ln, eps_rms = (sb(n, [P, 1]) for n in ("neg_half", "eps_ln", "eps_rms"))
        causal = sb("causal", [P, P], BF16)
        causal_t = sb("causal_t", [P, P], BF16)
        head_row = sb("head_row", [P, NH, P], BF16)
        parity = sb("parity", [P, 2])
        expert_row = sb("expert_row", [NE, EC, P])
        wa = sb("wa", [P, KC, 3, D])
        wo_a = sb("wo_a", [P, KC, D])
        wb = sb("wb", [P, KC, 5, D])
        wdn = sb("wdn", [P, KC, NE * BD + BD + NE])
        wup = sb("wup", [P, EC, D])
        wsu = sb("wsu", [BD, D])
        bu_sb = sb("bu_sb", [NE, D])
        vecs = sb("vecs", [P, 6 * KC + EC])
        g_col, b_col, nw_col = (vecs[:, i * KC:(i + 1) * KC] for i in range(3))
        bqkv = vecs[:, 3 * KC:6 * KC]
        bd_col = vecs[:, 6 * KC:]
        bfull = sb("bfull", [P, 3, KC])
        bq_par = sb("bq_par", [P, KC, 2])
        bsd_col = sb("bsd_col", [BD, 1])
        rows = sb("rows", [1, 2, D])
        bvb = sb("bvb", [P, KC, P])
        row_bc = sb("row_bc", [P, 2, D])
        mask_u8 = sb("mask_u8", [NB, P], U8)
        mask_f = sb("mask_f", [NB, P])
        valid = sb("valid", [P, NB])
        none_valid = sb("none_valid", [P, NB])
        key_cols = sb("key_cols", [P, NB, 3])

        x_in = [sb(f"x_in{i}", [P, D]) for i in range(2)]
        c_in = [sb(f"c_in{i}", [P, D]) for i in range(2)]
        x_bo = [sb(f"x_bo{i}", [P, D]) for i in range(2)]
        xn = sb("xn", [P, D])
        t1 = sb("t1", [P, 2, KC, P])
        t2 = sb("t2", [P, 2, KC, P])
        q_a, q_b = (sb(n, [P, KC, 2, P]) for n in ("q_a", "q_b"))
        k_a, k_b = (sb(n, [P, KC, P]) for n in ("k_a", "k_b"))
        v_a, v_b = (sb(n, [P, 8, 3, DH]) for n in ("v_a", "v_b"))
        den_a = sb("den_a", [P, 3, DH])
        den_b = [sb(f"den_b{i}", [P, 3, DH]) for i in range(2)]
        cols = [sb(f"cols{i}", [P, 3]) for i in range(2)]
        mdiag = [sb(f"mdiag{i}", [P, P], BF16) for i in range(2)]
        nm_a, nm_b = (sb(n, [P, NH], BF16) for n in ("nm_a", "nm_b"))
        nmt_a, nmt_b = (sb(n, [P, P], BF16) for n in ("nmt_a", "nmt_b"))
        e_a, e_b = (sb(n, [P, NR, 2, 2, P]) for n in ("e_a", "e_b"))
        rec_a, rec_b = (sb(n, [P, D]) for n in ("rec_a", "rec_b"))
        o_a, o_b = (sb(n, [P, KC, P]) for n in ("o_a", "o_b"))
        y_a, y_b, y_c = (sb(n, [P, D]) for n in ("y_a", "y_b", "y_c"))
        z_b = sb("z_b", [P, D])
        gate = sb("gate", [P, D])
        x1 = [sb(f"x1_{i}", [P, D]) for i in range(2)]
        xr = sb("xr", [P, D])
        x2 = sb("x2", [P, D])
        x2_b = sb("x2_b", [P, D])
        o_out = [sb(f"o_out{i}", [P, D]) for i in range(2)]
        st_x, st_a, st_b, st_c = (sb(n, [P, 6]) for n in ("st_x", "st_a", "st_b", "st_c"))
        mv_x, mv_a, mv_b, mv_c = (sb(n, [P, 2]) for n in ("mv_x", "mv_a", "mv_b", "mv_c"))
        ve_x, ve_a, ve_b, ve_c = (sb(n, [P, 1]) for n in ("ve_x", "ve_a", "ve_b", "ve_c"))
        rs_x, rs_a, rs_b, rs_c = (sb(n, [P, 1]) for n in ("rs_x", "rs_a", "rs_b", "rs_c"))
        rms = sb("rms", [P, 4])
        lg_t = sb("lg_t", [P, P])
        lg = sb("lg", [P, NE])
        rt = sb("rt", [P, 8, NE])
        rcol = sb("rcol", [P, 5])
        top8 = sb("top8", [P, 8])
        comb = sb("comb", [P, NE])
        comb_t = sb("comb_t", [NE, P])
        h = sb("h", [P, EC, P])
        hs = sb("hs", [BD, P])
        hc = sb("hc", [P, EC, P])

        S = es.enter_context(nc.psum_tensor("S", [P, NR, 2, 2, P], F32))
        G = [es.enter_context(nc.psum_tensor(f"G{i}", [P, 512], F32)) for i in range(4)]

        w_in = sem("w_in")
        x_ld = [sem(f"x_ld{i}") for i in range(2)]
        c_ld = [sem(f"c_ld{i}") for i in range(2)]
        out_st = [sem(f"out_st{i}") for i in range(2)]
        k_pool, k_dve, k_pe, k_ready = sem("k_pool"), sem("k_dve"), sem("k_pe"), sem("k_ready")
        (xn_mv, xn_ve, xn_rs, xn_ok, xbo_ok, t1_mm, t1_sb, qka_mm, qka_sb, va_mm, va_sb,
         sma_mm, nma_ok, mta_mm, mta_sb, sta_mm, ea_ok, oa_mm, ra_ok, oa_sb, woa_mm, ya_ok, mva_ok,
         vea_ok, rsa_ok, rm1, rm2, rm3, rm4, rma_ok, x1_ok, xr_ok) = (sem(n) for n in (
             "xn_mv xn_ve xn_rs xn_ok xbo_ok t1_mm t1_sb qka_mm qka_sb va_mm va_sb "
             "sma_mm nma_ok mta_mm mta_sb sta_mm ea_ok oa_mm ra_ok oa_sb woa_mm ya_ok mva_ok "
             "vea_ok rsa_ok rm1 rm2 rm3 rm4 rma_ok x1_ok xr_ok").split())
        (col_ok, bm_ok, tx_mm, tx_sb, qkb_mm, qkb_sb, vbg_mm, vbg_sb, smb_mm, nmb_ok, mtb_mm, mtb_sb,
         stb_mm, eb_ok, ob_mm, rb_ok, ob_sb, wob_mm, zb_ok, yb_ok, mvb_ok, veb_ok, rsb_ok,
         x2_ok, x2b_ok) = (sem(n) for n in (
             "col_ok bm_ok tx_mm tx_sb qkb_mm qkb_sb vbg_mm vbg_sb smb_mm nmb_ok mtb_mm mtb_sb "
             "stb_mm eb_ok ob_mm rb_ok ob_sb wob_mm zb_ok yb_ok mvb_ok veb_ok rsb_ok "
             "x2_ok x2b_ok").split())
        (ty_mm, ty_sb, dn2_mm, lgt_sb, dn1_mm, lt_mm, lg_ok, r1, r2, r3, r4, r5, r6, r7, r8, r9, rex_ok,
         comb_ok, ct_mm, ct_sb, h_ok, ce_mm, hc_ok, up_mm, yc_ok, mvc_ok, vec_ok, rsc_ok,
         out_ok) = (sem(n) for n in (
             "ty_mm ty_sb dn2_mm lgt_sb dn1_mm lt_mm lg_ok r1 r2 r3 r4 r5 r6 r7 r8 r9 rex_ok "
             "comb_ok ct_mm ct_sb h_ok ce_mm hc_ok up_mm yc_ok mvc_ok vec_ok rsc_ok "
             "out_ok").split())

        def wait(eng, signal, n):
            if isinstance(n, int):
                n = min(n, NB)
                if n <= 0:
                    return
            eng.wait_ge(signal, n)

        def schedule(eng, step):
            for s in (0, 1):
                step(s, s % 2)
            with eng.Fori(2, NB - 3, 2) as i:
                step(i, 0)
                step(i + 1, 1)
            for s in range(NB - 2, NB + 2):
                step(s, s % 2)

        def live(s, lag):
            return not isinstance(s, int) or 0 <= s - lag < NB

        block = es.enter_context(nc.Block())

        @block.sync
        def _(sp):
            def load_x(b, p):
                sp.dma_start(x_in[p][:, :], x[bass.ds(b, 1), :, :].rearrange("a t d -> (a t) d")).then_inc(x_ld[p], 16)

            def load_c(b, p):
                sp.dma_start(c_in[p][:, :], ctx_in[bass.ds(b, 1), :, :].rearrange("a t d -> (a t) d")).then_inc(c_ld[p], 16)

            load_x(0, 0)
            sp.dma_start(vecs[:, :], cols_in).then_inc(w_in, 16)
            sp.dma_start(wa[:, :, :, :], wa_in).then_inc(w_in, 16)
            load_c(0, 0)
            load_x(1, 1)
            sp.dma_start(wdn[:, :, :], wdn_in).then_inc(w_in, 16)
            sp.dma_start(wup[:, :, :], wup_in).then_inc(w_in, 16)

            def step(s, p):
                if not isinstance(s, int) or s + 2 < NB:
                    wait(sp, xn_ok, s + 1)
                    wait(sp, xbo_ok, s + 1)
                    load_x(s + 2, p)
                if not isinstance(s, int) or s + 1 < NB:
                    sp.wait_ge(t1_mm, s + 1)
                    load_c(s + 1, 1 - p)
                if live(s, 2):
                    wait(sp, out_ok, s - 1)
                    sp.dma_start(out[bass.ds(s - 2, 1), :, :].rearrange("a t d -> (a t) d"),
                                 o_out[p][:, :]).then_inc(out_st[p], 16)

            schedule(sp, step)
            for p in range(2):
                sp.wait_ge(out_st[p], 16 * NB // 2)

        @block.gpsimd
        def _(pool):
            gp = nc.gpsimd
            gp.memset(identf[:, :], 0.0)
            gp.memset(ones[:, :], 1.0)
            gp.memset(onesb[:, :], 1.0)
            gp.memset(neg_half[:, :], -0.5)
            gp.memset(eps_ln[:, :], EPS_LN)
            gp.memset(eps_rms[:, :], EPS_RMS)
            gp.memset(causal[:, :], 0.0)
            gp.memset(causal_t[:, :], 0.0)
            gp.memset(head_row[:, :, :], 1.0)
            gp.memset(expert_row[:, :, :], 0.0)
            gp.memset(den_a[:, :, :], 1.0)
            gp.memset(v_a[:, :, :, :], 0.0)
            gp.memset(v_b[:, :, :, :], 0.0)
            gp.memset(nmt_a[:, :], 0.0)
            gp.memset(nmt_b[:, :], 0.0)
            gp.memset(identb[:, :], 0.0).then_inc(k_pool, 1)
            pool.wait_ge(k_pool, 1)
            gp.affine_select(out=identf[:, :], in_=identf[:, :], compare_op=ALU.not_equal, fill=1.0,
                             base=0, pattern=[[-1, P]], channel_multiplier=1)
            gp.affine_select(out=identb[:, :], in_=identb[:, :], compare_op=ALU.not_equal, fill=1.0,
                             base=0, pattern=[[-1, P]], channel_multiplier=1)
            gp.affine_select(out=causal[:, :], in_=causal[:, :], compare_op=ALU.is_ge, fill=BIG,
                             base=0, pattern=[[-1, P]], channel_multiplier=1)
            gp.affine_select(out=causal_t[:, :], in_=causal_t[:, :], compare_op=ALU.is_ge, fill=BIG,
                             base=0, pattern=[[1, P]], channel_multiplier=-1)
            gp.affine_select(out=head_row[:, :, :], in_=head_row[:, :, :], compare_op=ALU.is_equal, fill=0.0,
                             base=0, pattern=[[1, NH], [0, P]], channel_multiplier=-1)
            gp.affine_select(out=expert_row[:, :, :].rearrange("e j (a b) -> e j a b", a=2),
                             in_=expert_row[:, :, :].rearrange("e j (a b) -> e j a b", a=2),
                             compare_op=ALU.not_equal, fill=1.0, base=0,
                             pattern=[[2, EC], [1, 2], [0, BD]], channel_multiplier=-1)
            gp.memset(den_a[:, 1:2, :], 0.0)
            for i in range(2):
                gp.memset(den_b[i][:, :, :], 0.0)
            gp.memset(cols[0][:, :], 0.0).then_inc(k_pool, 1)
            pool.wait_ge(k_ready, 1)

            def rstd(ve, mv, rs, mv_ok, ve_ok, rs_ok, n, eps):
                wait(pool, mv_ok, n)
                gp.tensor_tensor(ve[:, :], mv[:, 1:2], eps, ALU.add).then_inc(ve_ok, 1)
                wait(pool, ve_ok, n)
                gp.tensor_tensor(rs[:, :], ve[:, :], neg_half[:, :], ALU.pow).then_inc(rs_ok, 1)

            def first(n, p):
                rstd(ve_x, mv_x, rs_x, xn_mv, xn_ve, xn_rs, n, eps_ln[:, :])
                wait(pool, ya_ok, n - 2)
                gp.tensor_tensor(x_bo[p][:, :], x_in[p][:, :], row_bc[:, 0, :], ALU.add).then_inc(xbo_ok, 1)

            first(1, 0)

            def step(s, p):
                if live(s, 2):
                    rstd(ve_b, mv_b, rs_b, mvb_ok, veb_ok, rsb_ok, s - 1, eps_ln[:, :])
                if live(s, 0):
                    wait(pool, ob_mm, s - 1)
                    gp.tensor_copy(cols[p][:, :], key_cols[:, bass.ds(s, 1), :].rearrange("p a c -> p (a c)")).then_inc(col_ok, 1)
                    wait(pool, col_ok, s + 1)
                    gp.tensor_tensor(mdiag[p][:, :], identb[:, :], cols[p][:, 2:3].to_broadcast([P, P]), ALU.mult)
                    gp.tensor_scalar(den_b[p][:, 0::2, :], den_a[:, 0::2, :], cols[p][:, 1:2], None,
                                     ALU.mult).then_inc(bm_ok, 1)
                if live(s, 2):
                    wait(pool, x2_ok, s - 1)
                    wait(pool, yc_ok, s - 2)
                    gp.tensor_tensor(x2_b[:, :], x2[:, :], row_bc[:, 1, :], ALU.add).then_inc(x2b_ok, 1)
                    rstd(ve_c, mv_c, rs_c, mvc_ok, vec_ok, rsc_ok, s - 1, eps_ln[:, :])
                if not isinstance(s, int) or s + 1 < NB:
                    first(s + 2, 1 - p)
                if live(s, 0):
                    rstd(ve_a, mv_a, rs_a, mva_ok, vea_ok, rsa_ok, s + 1, eps_ln[:, :])
                    wait(pool, rsa_ok, s + 1)
                    gp.tensor_tensor(rms[:, 0:1], mv_a[:, 1:2], rs_a[:, :], ALU.mult).then_inc(rm1, 1)
                    wait(pool, rm1, s + 1)
                    gp.tensor_tensor(rms[:, 1:2], rms[:, 0:1], rs_a[:, :], ALU.mult).then_inc(rm2, 1)
                    wait(pool, rm2, s + 1)
                    gp.tensor_tensor(rms[:, 2:3], rms[:, 1:2], eps_rms[:, :], ALU.add).then_inc(rm3, 1)
                    wait(pool, rm3, s + 1)
                    gp.tensor_tensor(rms[:, 3:4], rms[:, 2:3], neg_half[:, :], ALU.pow).then_inc(rma_ok, 1)

            schedule(pool, step)

        @block.scalar
        def _(act):
            ac = nc.scalar
            act.dma_start(mask_u8[:, :], mask).then_inc(w_in, 16)
            act.dma_start(rows[:, :, :], rows_in).then_inc(w_in, 16)
            act.dma_start(bsd_col[:, :], bsd_in).then_inc(w_in, 16)
            act.dma_start(wo_a[:, :, :], wo_a_in).then_inc(w_in, 16)
            act.dma_start(wb[:, :, :, :], wb_in).then_inc(w_in, 16)
            act.dma_start(wsu[:, :], wsu_in).then_inc(w_in, 16)
            act.dma_start(bu_sb[:, :], bu_in).then_inc(w_in, 16)
            act.wait_ge(w_in, 16 * WEIGHTS)

            def step(s, p):
                A, B, B2 = live(s, 0), live(s, 1), live(s, 2)
                if A or B:
                    act.wait_ge(t1_mm, s + 1)
                    wait(act, vbg_mm, s - 1)
                    wait(act, va_mm, s)
                    if A and B:
                        ac.activation(t1[:, :, :, :].rearrange("p a k t -> p (a k t)"), G[0][:, :], ACT.Copy).then_inc(t1_sb, 1)
                    elif A:
                        ac.activation(t1[:, 0, :, :].rearrange("p k t -> p (k t)"), G[0][:, 0:256], ACT.Copy).then_inc(t1_sb, 1)
                    else:
                        ac.activation(t1[:, 1, :, :].rearrange("p k t -> p (k t)"), G[0][:, 256:512], ACT.Copy).then_inc(t1_sb, 1)
                if A:
                    wait(act, va_mm, s + 1)
                    wait(act, oa_mm, s)
                    ac.activation(v_a[:, :, 0::2, :], G[2][:, 0:256].rearrange("p (a b d) -> p a b d", b=2, d=DH),
                                  ACT.Copy).then_inc(va_sb, 1)
                if B:
                    wait(act, tx_mm, s)
                    wait(act, vbg_mm, s - 1)
                    ac.activation(t2[:, 0, :, :].rearrange("p k t -> p (k t)"), G[2][:, 0:256], ACT.Copy).then_inc(tx_sb, 1)
                    wait(act, vbg_mm, s)
                    wait(act, bm_ok, s)
                    wait(act, ob_mm, s - 1)
                    ac.activation(v_b[:, :, 0::2, :], G[3][:, 0:256].rearrange("p (a b d) -> p a b d", b=2, d=DH),
                                  ACT.Copy, scale=cols[1 - p][:, 0:1])
                    wait(act, zb_ok, s - 1)
                    ac.activation(gate[:, :], G[3][:, 256:512], ACT.Tanh, scale=0.5).then_inc(vbg_sb, 1)
                if B2:
                    wait(act, ty_mm, s - 1)
                    wait(act, dn1_mm, s - 2)
                    ac.activation(t2[:, 1, :, :].rearrange("p k t -> p (k t)"), G[2][:, 0:256], ACT.Copy).then_inc(ty_sb, 1)
                    wait(act, dn2_mm, s - 1)
                    wait(act, lt_mm, s - 2)
                    ac.activation(lg_t[BD:BD + NE, :], G[3][BD:BD + NE, 0:P], ACT.Copy).then_inc(lgt_sb, 1)
                if A:
                    wait(act, mta_mm, s + 1)
                    wait(act, sta_mm, s)
                    ac.activation(nmt_a[0:NH, :], G[2][0:NH, 0:64].bitcast(BF16), ACT.Copy).then_inc(mta_sb, 1)
                if B2:
                    wait(act, r1, s - 1)
                    ac.activation(rt[:, 0, :], lg[:, :], ACT.Exp, bias=rcol[:, 1:2]).then_inc(rex_ok, 1)
                    wait(act, dn1_mm, s - 1)
                    wait(act, up_mm, s - 2)
                    wait(act, hc_ok, s - 2)
                    ac.activation(hs[:, :], G[3][0:BD, 0:P], ACT.Gelu, bias=bsd_col[:, :])
                    for j in range(EC):
                        last = ac.activation(h[:, j, :], G[0][:, j * P:(j + 1) * P], ACT.Gelu, bias=bd_col[:, j:j + 1])
                    last.then_inc(h_ok, 1)
                if A:
                    wait(act, sta_mm, s + 1)
                    wait(act, oa_mm, s)
                    ac.activation(e_a[:, :, :, :, :].rearrange("p r c a q -> p (r c a q)"),
                                  S[:, :, :, :, :].rearrange("p r c a q -> p (r c a q)"), ACT.Exp,
                                  scale=SCALE).then_inc(ea_ok, 1)
                if B:
                    wait(act, mtb_mm, s)
                    wait(act, stb_mm, s - 1)
                    ac.activation(nmt_b[0:NH, :], G[2][0:NH, 0:64].bitcast(BF16), ACT.Copy).then_inc(mtb_sb, 1)
                    wait(act, stb_mm, s)
                    wait(act, ob_mm, s - 1)
                    ac.activation(e_b[:, :, :, :, :].rearrange("p r c a q -> p (r c a q)"),
                                  S[:, :, :, :, :].rearrange("p r c a q -> p (r c a q)"), ACT.Exp,
                                  scale=SCALE, bias=cols[1 - p][:, 2:3]).then_inc(eb_ok, 1)

            schedule(act, step)

        @block.vector
        def _(dve):
            v = nc.vector
            chain = [0]

            def link(ins):
                chain[0] += 1
                ins.then_inc(k_dve, 1)
                dve.wait_ge(k_dve, chain[0])

            dve.wait_ge(w_in, 16 * WEIGHTS)
            dve.wait_ge(k_pool, 2)
            v.reduce_sum(parity[:, :], identf[:, :].rearrange("p (r a d) -> p a r d", a=2, d=DH), axis=AX.XY)
            link(v.tensor_copy(mask_f[:, :], mask_u8[:, :]))
            dve.wait_ge(k_pe, 1)
            v.tensor_copy(valid[:, :], G[0][:, 0:NB])
            link(v.tensor_tensor(bfull[:, :, :].rearrange("p a k -> p (a k)"), G[1][:, 0:6],
                                 bqkv, ALU.add))
            for k in range(KC):
                v.tensor_scalar(bq_par[:, k, :], parity[:, :], bfull[:, 0, k:k + 1], None, ALU.mult)
                v.tensor_scalar(bvb[:, k, :], ones[:, :], bfull[:, 2, k:k + 1], None, ALU.mult)
                v.tensor_scalar(wa[:, k, :, :].rearrange("p a n -> p (a n)"), wa[:, k, :, :].rearrange("p a n -> p (a n)"),
                                g_col[:, k:k + 1], None, ALU.mult)
                v.tensor_scalar(wb[:, k, 0:2, :].rearrange("p a n -> p (a n)"), wb[:, k, 0:2, :].rearrange("p a n -> p (a n)"),
                                nw_col[:, k:k + 1], None, ALU.mult)
                v.tensor_scalar(wb[:, k, 4, :], wb[:, k, 4, :], 0.5, None, ALU.mult)
            link(v.tensor_copy(key_cols[:, :, 0], valid[:, :]))
            dve.wait_ge(k_pe, 2)
            link(v.tensor_scalar(none_valid[:, :], G[2][:, 0:NB], 0.5, None, ALU.is_lt))
            link(v.tensor_tensor(key_cols[:, :, 1], none_valid[:, :], valid[:, :], ALU.max))
            v.tensor_scalar(key_cols[:, :, 2], key_cols[:, :, 1], -BIG, BIG, ALU.mult, ALU.add)
            v.tensor_copy(row_bc[:, :, :].rearrange("p a n -> p (a n)"), G[3][:, :]).then_inc(k_ready, 1)

            def stats(y, st, mv, mv_ok):
                v.bn_stats(st[:, :], y)
                dve.drain()
                v.bn_aggr(mv[:, :], st[:, :]).then_inc(mv_ok, 1)

            def first_norm(n, p, loaded):
                dve.wait_ge(x_ld[p], loaded)
                stats(x_in[p][:, :], st_x, mv_x, xn_mv)
                wait(dve, xn_rs, n)
                if not isinstance(n, int) or n > 1:
                    dve.wait_ge(t1_mm, n - 1)
                v.tensor_scalar(xn[:, :], x_in[p][:, :], mv_x[:, 0:1], rs_x[:, :], ALU.subtract, ALU.mult).then_inc(xn_ok, 1)

            first_norm(1, 0, 16)

            def step(s, p):
                A, B, B2 = live(s, 0), live(s, 1), live(s, 2)
                if A:
                    wait(dve, qka_mm, s + 1)
                    wait(dve, sta_mm, s)
                    for c in range(KC):
                        for a in range(2):
                            v.tensor_scalar(q_a[:, c, a, :], G[1][:, c * P:(c + 1) * P], parity[:, a:a + 1],
                                            bq_par[:, c, a:a + 1], ALU.mult, ALU.add)
                        last = v.tensor_scalar(k_a[:, c, :], G[1][:, 256 + c * P:256 + (c + 1) * P],
                                               bfull[:, 1, c:c + 1], None, ALU.add)
                    last.then_inc(qka_sb, 1)
                if B2:
                    wait(dve, ob_mm, s - 1)
                    v.reciprocal(rec_b[:, :], G[3][:, 256:512]).then_inc(rb_ok, 1)
                    wait(dve, rb_ok, s - 1)
                    wait(dve, wob_mm, s - 2)
                    v.tensor_tensor(o_b[:, :, :].rearrange("p c t -> p (c t)"), G[3][:, 0:256], rec_b[:, :], ALU.mult).then_inc(ob_sb, 1)
                    wait(dve, wob_mm, s - 1)
                    v.scalar_tensor_tensor(out=z_b[:, :], in0=gate[:, :], scalar=1.0, in1=G[0][:, 0:256],
                                           op0=ALU.add, op1=ALU.mult).then_inc(zb_ok, 1)
                    wait(dve, zb_ok, s - 1)
                    v.tensor_tensor(y_b[:, :], z_b[:, :], x1[p][:, :], ALU.add).then_inc(yb_ok, 1)
                    wait(dve, yb_ok, s - 1)
                    stats(y_b[:, :], st_b, mv_b, mvb_ok)
                if B:
                    wait(dve, qkb_mm, s)
                    wait(dve, stb_mm, s - 1)
                    for a in range(2):
                        v.tensor_scalar(q_b[:, :, a, :], G[1][:, 0:256].rearrange("p (c t) -> p c t", c=KC),
                                        parity[:, a:a + 1], None, ALU.mult)
                    v.tensor_copy(k_b[:, :, :].rearrange("p c t -> p (c t)"), G[1][:, 256:512]).then_inc(qkb_sb, 1)
                if B2:
                    wait(dve, rsb_ok, s - 1)
                    wait(dve, ty_mm, s - 2)
                    wait(dve, x2b_ok, s - 2)
                    v.tensor_scalar(x2[:, :], y_b[:, :], mv_b[:, 0:1], rs_b[:, :], ALU.subtract, ALU.mult).then_inc(x2_ok, 1)
                if A:
                    wait(dve, sma_mm, s + 1)
                    v.tensor_reduce(nm_a[:, :], S[:, :, :, :, :].rearrange("p r c a k -> p (r c a) k"),
                                    op=ALU.max, axis=AX.X, negate=True).then_inc(nma_ok, 1)
                if B2:
                    wait(dve, lt_mm, s - 1)
                    v.tensor_copy(lg[:, :], G[1][:, 0:NE]).then_inc(lg_ok, 1)
                    wait(dve, lg_ok, s - 1)
                    v.reduce_max(rcol[:, 0:1], lg[:, :], axis=AX.X).then_inc(r2, 1)
                    wait(dve, r2, s - 1)
                    v.tensor_scalar(rcol[:, 1:2], rcol[:, 0:1], -1.0, None, ALU.mult).then_inc(r1, 1)
                    v.tensor_scalar(rt[:, 1, :], lg[:, :], rcol[:, 0:1], None, ALU.is_equal).then_inc(r3, 1)
                    wait(dve, r3, s - 1)
                    v.tensor_tensor_scan(rt[:, 2, :], ones[:, 0:NE], rt[:, 1, :], 0.0, ALU.mult, ALU.add).then_inc(r4, 1)
                    wait(dve, r4, s - 1)
                    v.scalar_tensor_tensor(out=rt[:, 3, :], in0=rt[:, 2, :], scalar=1.0, in1=rt[:, 1, :],
                                           op0=ALU.is_equal, op1=ALU.mult).then_inc(r5, 1)
                    wait(dve, r5, s - 1)
                    v.scalar_tensor_tensor(out=rt[:, 4, :], in0=rt[:, 3, :], scalar=3.0 * BIG, in1=lg[:, :],
                                           op0=ALU.mult, op1=ALU.add).then_inc(r6, 1)
                    wait(dve, r6, s - 1)
                    v.reduce_max(rcol[:, 2:3], rt[:, 4, :], axis=AX.X).then_inc(r7, 1)
                    wait(dve, r7, s - 1)
                    v.tensor_scalar(rt[:, 5, :], rt[:, 4, :], rcol[:, 2:3], None, ALU.is_equal).then_inc(r8, 1)
                    wait(dve, r8, s - 1)
                    v.tensor_tensor_scan(rt[:, 6, :], ones[:, 0:NE], rt[:, 5, :], 0.0, ALU.mult, ALU.add).then_inc(r9, 1)
                    wait(dve, r9, s - 1)
                    router_tail(s)
                    wait(dve, ct_mm, s - 1)
                    wait(dve, up_mm, s - 2)
                    v.tensor_copy(comb_t[:, :], G[1][0:NE, 0:P]).then_inc(ct_sb, 1)
                    wait(dve, ce_mm, s - 1)
                    wait(dve, h_ok, s - 1)
                    v.tensor_tensor(hc[:, :, :].rearrange("p j t -> p (j t)"), h[:, :, :].rearrange("p j t -> p (j t)"),
                                    G[0][:, :], ALU.mult).then_inc(hc_ok, 1)
                if B:
                    wait(dve, smb_mm, s)
                    v.tensor_reduce(nm_b[:, :], S[:, :, :, :, :].rearrange("p r c a k -> p (r c a) k"),
                                    op=ALU.max, axis=AX.X, negate=True).then_inc(nmb_ok, 1)
                if B2:
                    wait(dve, up_mm, s - 1)
                    wait(dve, x2b_ok, s - 1)
                    v.tensor_tensor(y_c[:, :], G[3][:, 0:256], x2_b[:, :], ALU.add).then_inc(yc_ok, 1)
                    wait(dve, yc_ok, s - 1)
                    stats(y_c[:, :], st_c, mv_c, mvc_ok)
                if A:
                    wait(dve, oa_mm, s + 1)
                    v.reciprocal(rec_a[:, :], G[1][:, 256:512]).then_inc(ra_ok, 1)
                    wait(dve, ra_ok, s + 1)
                    v.tensor_tensor(o_a[:, :, :].rearrange("p c t -> p (c t)"), G[1][:, 0:256], rec_a[:, :], ALU.mult).then_inc(oa_sb, 1)
                if B2:
                    wait(dve, rsc_ok, s - 1)
                    if not isinstance(s, int) or s >= 4:
                        dve.wait_ge(out_st[p], 8 * s - 16 - 8 * p)
                    v.tensor_scalar(o_out[p][:, :], y_c[:, :], mv_c[:, 0:1], rs_c[:, :], ALU.subtract, ALU.mult).then_inc(out_ok, 1)
                if not isinstance(s, int) or s + 1 < NB:
                    first_norm(s + 2, 1 - p, 8 * (s + 1) + 16 - 8 * (1 - p))
                if A:
                    wait(dve, woa_mm, s + 1)
                    wait(dve, xbo_ok, s + 1)
                    v.tensor_tensor(y_a[:, :], G[0][:, 0:256], x_bo[p][:, :], ALU.add).then_inc(ya_ok, 1)
                    wait(dve, ya_ok, s + 1)
                    stats(y_a[:, :], st_a, mv_a, mva_ok)
                    wait(dve, rsa_ok, s + 1)
                    v.tensor_scalar(x1[p][:, :], y_a[:, :], mv_a[:, 0:1], rs_a[:, :], ALU.subtract, ALU.mult).then_inc(x1_ok, 1)
                    wait(dve, x1_ok, s + 1)
                    wait(dve, rma_ok, s + 1)
                    wait(dve, tx_mm, s)
                    v.tensor_scalar(xr[:, :], x1[p][:, :], rms[:, 3:4], None, ALU.mult).then_inc(xr_ok, 1)

            def router_tail(s):
                v.scalar_tensor_tensor(out=rt[:, 7, :], in0=rt[:, 6, :], scalar=1.0, in1=rt[:, 5, :],
                                       op0=ALU.is_equal, op1=ALU.mult).then_inc(t_sel, 1)
                wait(dve, t_sel, s - 1)
                v.tensor_tensor(rt[:, 5, :], rt[:, 7, :], rt[:, 3, :], ALU.add).then_inc(t_both, 1)
                wait(dve, t_both, s - 1)
                wait(dve, rex_ok, s - 1)
                v.tensor_tensor(rt[:, 1, :], rt[:, 5, :], rt[:, 0, :], ALU.mult).then_inc(t_mul, 1)
                wait(dve, t_mul, s - 1)
                v.reduce_sum(rcol[:, 3:4], rt[:, 1, :], axis=AX.X).then_inc(t_sum, 1)
                wait(dve, t_sum, s - 1)
                v.reciprocal(rcol[:, 4:5], rcol[:, 3:4]).then_inc(t_rec, 1)
                wait(dve, t_rec, s - 1)
                v.tensor_scalar(comb[:, :], rt[:, 1, :], rcol[:, 4:5], None, ALU.mult).then_inc(comb_ok, 1)

            t_sel, t_both, t_mul, t_sum, t_rec = (sem(n) for n in ("t_sel", "t_both", "t_mul", "t_sum", "t_rec"))
            schedule(dve, step)

        @block.tensor
        def _(pe):
            mm = nc.tensor.matmul

            pe.wait_ge(k_pool, 2)
            pe.wait_ge(w_in, 16 * WEIGHTS)
            pe.wait_ge(k_dve, 1)
            nc.tensor.transpose(G[0][:, 0:NB], mask_f[:, :], identf[0:NB, 0:NB])
            for i in range(3):
                for m in range(KC):
                    for k in range(KC):
                        last = mm(G[1][:, i * KC + m:i * KC + m + 1], wa[:, k, i, m * P:(m + 1) * P], b_col[:, k:k + 1],
                                  start=(k == 0), stop=(k == KC - 1))
            last.then_inc(k_pe, 1)
            pe.wait_ge(k_dve, 3)
            mm(G[2][:, 0:NB], ones[:, :], valid[:, :], start=True, stop=True)
            mm(G[3][:, 0:D], ones[0:1, :], rows[:, 0, :], start=True, stop=False)
            for k in range(KC):
                mm(G[3][:, 0:D], bvb[:, k, :], wo_a[:, k, :], start=False, stop=(k == KC - 1))
            mm(G[3][:, D:2 * D], ones[0:1, :], rows[:, 1, :], start=True, stop=True).then_inc(k_pe, 1)
            pe.wait_ge(k_ready, 1)

            def project_t(dst, w, i, src, a):
                for m in range(KC):
                    for k in range(KC):
                        last = mm(dst[:, m * P:(m + 1) * P], w[:, k, i, m * P:(m + 1) * P], src[:, a, k, :],
                                  start=(k == 0), stop=(k == KC - 1))
                return last

            def project(dst, src, w, i):
                for k in range(KC):
                    last = mm(dst, src[:, k, :], w[:, k, i, :], start=(k == 0), stop=(k == KC - 1))
                return last

            def high(t):
                return t.bitcast(BF16)

            def scores_for_max(q, k, mask_l, mask_r):
                for r in range(NR):
                    mm(S[:, r, :, :, :].rearrange("p c a k -> p (c a) k"), mask_l,
                       mask_r.unsqueeze(1).to_broadcast([P, 4, P]), start=True, stop=False, skip_group_check=True)
                for c in range(KC):
                    for a in range(2):
                        for r in range(NR):
                            g = slice(32 * r, 32 * r + 32)
                            last = mm(S[:, r, c, a, :], high(q[g, c, a, :])[:, 1::2], high(k[g, c, :])[:, 1::2],
                                      start=False, stop=True, skip_group_check=True)
                return last

            def scores_t(q, k, nmt, causal_too):
                for r in range(NR):
                    if causal_too:
                        mm(S[:, r, :, :, :].rearrange("p c a q -> p (c a) q"), identb[:, :],
                           causal_t[:, :].unsqueeze(1).to_broadcast([P, 4, P]), start=True, stop=False,
                           skip_group_check=True)
                    for c in range(KC):
                        for a in range(2):
                            mm(S[:, r, c, a, :], head_row[:, 4 * r + 2 * c + a, :], nmt[:, :],
                               start=(not causal_too and c == 0 and a == 0), stop=False, skip_group_check=True)
                for c in range(KC):
                    for r in range(NR):
                        g = slice(32 * r, 32 * r + 32)
                        last = mm(S[:, r, c, :, :], k[g, c, :], q[g, c, :, :], start=False, stop=True,
                                  skip_group_check=True)
                return last

            def values(dst, v_, e, den):
                for c in range(KC):
                    for a in range(2):
                        for r in range(NR):
                            mm(dst[32 * r:32 * r + 32, c * P:(c + 1) * P],
                               v_[:, 4 * c + r, a:a + 2, :].rearrange("p a d -> p (a d)"), e[:, r, c, a, :],
                               start=(a == 0), stop=(a == 1))
                for a in range(2):
                    for r in range(NR):
                        last = mm(dst[32 * r:32 * r + 32, 256:512].rearrange("p (c q) -> p c q", c=KC),
                                  den[:, a:a + 2, :].rearrange("p a d -> p (a d)"), e[:, r, :, a, :],
                                  start=(a == 0), stop=(a == 1))
                return last

            def step(s, p):
                A, B, B2 = live(s, 0), live(s, 1), live(s, 2)
                if A or B:
                    wait(pe, ya_ok, s)
                    if A:
                        wait(pe, xn_ok, s + 1)
                        for k in range(KC):
                            last = nc.tensor.transpose(G[0][:, k * P:(k + 1) * P], xn[:, k * P:(k + 1) * P], identf[:, :])
                    if B:
                        pe.wait_ge(c_ld[1 - p], 8 * (s - 1) + 16 - 8 * (1 - p))
                        for k in range(KC):
                            last = nc.tensor.transpose(G[0][:, 256 + k * P:256 + (k + 1) * P],
                                                       c_in[1 - p][:, k * P:(k + 1) * P], identf[:, :])
                    last.then_inc(t1_mm, 1)
                if A:
                    wait(pe, oa_sb, s)
                    wait(pe, t1_sb, s + 1)
                    project_t(G[1][:, 0:256], wa, 0, t1, 0)
                    project_t(G[1][:, 256:512], wa, 1, t1, 0).then_inc(qka_mm, 1)
                    wait(pe, mtb_sb, s - 1)
                    project(G[2][:, 0:256], t1[:, 0, :, :], wa, 2).then_inc(va_mm, 1)
                if B2:
                    wait(pe, eb_ok, s - 1)
                    wait(pe, yc_ok, s - 2)
                    values(G[3], v_b, e_b, den_b[p]).then_inc(ob_mm, 1)
                    wait(pe, ob_sb, s - 1)
                    if A or B:
                        pe.wait_ge(t1_sb, s + 1)
                    project(G[0][:, 0:256], o_b, wb, 4).then_inc(wob_mm, 1)
                if B:
                    wait(pe, va_sb, s + 1)
                    wait(pe, xr_ok, s)
                    for k in range(KC):
                        last = nc.tensor.transpose(G[2][:, k * P:(k + 1) * P], xr[:, k * P:(k + 1) * P], identf[:, :])
                    last.then_inc(tx_mm, 1)
                    wait(pe, tx_sb, s)
                    wait(pe, qka_sb, s + 1)
                    project_t(G[1][:, 0:256], wb, 0, t2, 0)
                    project_t(G[1][:, 256:512], wb, 2, t1, 1).then_inc(qkb_mm, 1)
                    wait(pe, ob_sb, s - 1)
                    project(G[3][:, 0:256], t1[:, 1, :, :], wb, 3)
                    project(G[3][:, 256:512], t2[:, 0, :, :], wb, 1).then_inc(vbg_mm, 1)
                if A:
                    wait(pe, qka_sb, s + 1)
                    wait(pe, eb_ok, s - 1)
                    scores_for_max(q_a, k_a, identb[:, :], causal[:, :]).then_inc(sma_mm, 1)
                if B2:
                    wait(pe, x2_ok, s - 1)
                    wait(pe, tx_sb, s)
                    for k in range(KC):
                        last = nc.tensor.transpose(G[2][:, k * P:(k + 1) * P], x2[:, k * P:(k + 1) * P], identf[:, :])
                    last.then_inc(ty_mm, 1)
                    wait(pe, ty_sb, s - 1)
                    wait(pe, vbg_sb, s)
                    for k in range(KC):
                        last = mm(G[3][0:BD + NE, 0:P], wdn[:, k, NE * BD:], t2[:, 1, k, :], start=(k == 0), stop=(k == KC - 1))
                    last.then_inc(dn2_mm, 1)
                    wait(pe, zb_ok, s - 1)
                    for j in range(EC):
                        for k in range(KC):
                            last = mm(G[0][:, j * P:(j + 1) * P], wdn[:, k, j * P:(j + 1) * P], t2[:, 1, k, :],
                                      start=(k == 0), stop=(k == KC - 1))
                    last.then_inc(dn1_mm, 1)
                    wait(pe, lgt_sb, s - 1)
                    wait(pe, qkb_sb, s)
                    mm(G[1][:, 0:NE], lg_t[BD:BD + NE, :], identf[BD:BD + NE, BD:BD + NE], start=True, stop=True).then_inc(lt_mm, 1)
                if A:
                    wait(pe, nma_ok, s + 1)
                    wait(pe, va_sb, s + 1)
                    wait(pe, tx_sb, s)
                    wait(pe, ty_sb, s - 1)
                    nc.tensor.transpose(G[2][0:NH, 0:64].bitcast(BF16), nm_a[:, :], identb[:, :]).then_inc(mta_mm, 1)
                    wait(pe, mta_sb, s + 1)
                    scores_t(q_a, k_a, nmt_a, True).then_inc(sta_mm, 1)
                if B2:
                    wait(pe, comb_ok, s - 1)
                    wait(pe, lg_ok, s - 1)
                    nc.tensor.transpose(G[1][0:NE, 0:P], comb[:, :], identf[:, :]).then_inc(ct_mm, 1)
                    wait(pe, ct_sb, s - 1)
                    wait(pe, h_ok, s - 1)
                    for j in range(EC):
                        last = mm(G[0][:, j * P:(j + 1) * P], expert_row[:, j, :], comb_t[:, :], start=True, stop=True)
                    last.then_inc(ce_mm, 1)
                    wait(pe, hc_ok, s - 1)
                    mm(G[3][:, 0:256], comb_t[:, :], bu_sb[:, :], start=True, stop=False)
                    mm(G[3][:, 0:256], hs[:, :], wsu[:, :], start=False, stop=False)
                    for j in range(EC):
                        last = mm(G[3][:, 0:256], hc[:, j, :], wup[:, j, :], start=False, stop=(j == EC - 1))
                    last.then_inc(up_mm, 1)
                if B:
                    wait(pe, ea_ok, s + 1)
                    wait(pe, qkb_sb, s)
                    wait(pe, bm_ok, s)
                    scores_for_max(q_b, k_b, onesb[:, :], mdiag[1 - p][:, :]).then_inc(smb_mm, 1)
                if A:
                    wait(pe, ea_ok, s + 1)
                    wait(pe, va_sb, s + 1)
                    wait(pe, qkb_sb, s)
                    wait(pe, ct_sb, s - 1)
                    values(G[1], v_a, e_a, den_a).then_inc(oa_mm, 1)
                if B:
                    wait(pe, nmb_ok, s)
                    wait(pe, mta_sb, s + 1)
                    nc.tensor.transpose(G[2][0:NH, 0:64].bitcast(BF16), nm_b[:, :], identb[:, :]).then_inc(mtb_mm, 1)
                    wait(pe, mtb_sb, s)
                    scores_t(q_b, k_b, nmt_b, False).then_inc(stb_mm, 1)
                if A:
                    wait(pe, oa_sb, s + 1)
                    wait(pe, hc_ok, s - 1)
                    for k in range(KC):
                        last = mm(G[0][:, 0:256], o_a[:, k, :], wo_a[:, k, :], start=(k == 0), stop=(k == KC - 1))
                    last.then_inc(woa_mm, 1)

            schedule(pe, step)


_OUT = ((NB, P, D), "float32")


def kernel(x, ctx_2048, mask_BxS2_bk0, L0_attn_ln_g, L0_attn_ln_b, L0_attn_Wq, L0_attn_bq, L0_attn_Wk,
           L0_attn_bk, L0_attn_Wv, L0_attn_bv, L0_attn_Wo, L0_attn_bo, L0_xattn_norm_w, L0_xattn_wq,
           L0_xattn_wk, L0_xattn_wv, L0_xattn_wo, L0_xattn_wg, L0_ffn_gate_w, L0_ffn_wd, L0_ffn_bd,
           L0_ffn_wu, L0_ffn_bu, L0_ffn_ws_d, L0_ffn_bs_d, L0_ffn_ws_u, L0_ffn_bs_u):
    import numpy as np
    import concourse.bacc as bacc
    from concourse.bass_utils import run_bass_kernel_spmd

    A = np.asarray

    def k_rows(*ws):
        w = np.concatenate(ws, axis=1)
        return w.reshape(-1, P, w.shape[1]).transpose(1, 0, 2)

    def columns(*vs):
        return np.concatenate([A(v).reshape(-1, P) for v in vs]).T

    wd, wu = A(L0_ffn_wd), A(L0_ffn_wu)
    laid_out = [
        ("x", A(x)), ("ctx", A(ctx_2048)), ("mask", A(mask_BxS2_bk0)),
        ("vectors", columns(L0_attn_ln_g, L0_attn_ln_b, L0_xattn_norm_w, L0_attn_bq, L0_attn_bk, L0_attn_bv,
                            L0_ffn_bd)),
        ("rows", np.stack([A(L0_attn_bo), A(L0_ffn_bs_u)])[None]),
        ("wa", k_rows(A(L0_attn_Wq), A(L0_attn_Wk), A(L0_attn_Wv)).reshape(P, KC, 3, D)),
        ("wo_a", k_rows(A(L0_attn_Wo))),
        ("wb", k_rows(A(L0_xattn_wq).T, A(L0_xattn_wg).T, A(L0_xattn_wk).T, A(L0_xattn_wv).T,
                      A(L0_xattn_wo).T).reshape(P, KC, 5, D)),
        ("wdn", k_rows(wd.reshape(-1, D).T, A(L0_ffn_ws_d).T, A(L0_ffn_gate_w).T)),
        ("wup", k_rows(wu.transpose(0, 2, 1).reshape(-1, D))),
        ("wsu", A(L0_ffn_ws_u).T), ("bu", A(L0_ffn_bu)), ("bsd", A(L0_ffn_bs_d)[:, None]),
    ]
    nc = bacc.Bacc("TRN2", target_bir_lowering=False, num_devices=1)
    arrays, args = {}, []
    for name, a in laid_out:
        a = np.ascontiguousarray(a)
        arrays[f"in_{name}"] = a
        args.append(nc.dram_tensor(f"in_{name}", a.shape, mybir.dt.from_np(a.dtype), kind="ExternalInput").ap())
    out = nc.dram_tensor("out", _OUT[0], mybir.dt.from_np(np.dtype(_OUT[1])), kind="ExternalOutput").ap()
    decoder_layer(nc, *args, out)
    r = run_bass_kernel_spmd(nc, [arrays], core_ids=[0])
    return r.results[0]["out"]
```

```python
import concourse.bass as bass
from concourse import mybir
from contextlib import ExitStack

F32 = mybir.dt.float32
BF16 = mybir.dt.bfloat16
U8 = mybir.dt.uint8
ALU = mybir.AluOpType
ACT = mybir.ActivationFunctionType
AX = mybir.AxisListType

NB = 16
P = 128
D = 256
KC = D // P
NH = 16
DH = D // NH
NR = 4
NE = 8
BD = 64
EC = NE * BD // P
SCALE = DH ** -0.5
BIG = -1.0e30
EPS_LN = 1e-5
EPS_RMS = 1e-6
WEIGHTS = 10


def decoder_layer(nc, x, ctx_in, mask, cols_in, rows_in, wa_in, wo_a_in, wb_in, wdn_in, wup_in, wsu_in,
                  bsd_in, out):
    es = ExitStack()
    with es:
        def sb(name, shape, dt=F32):
            return es.enter_context(nc.sbuf_tensor(name, shape, dt))

        def sem(name):
            return es.enter_context(nc.semaphore(name))

        identf = sb("identf", [P, P])
        identb = sb("identb", [P, P], BF16)
        ones = sb("ones", [P, P])
        onesb = sb("onesb", [P, P], BF16)
        neg_half, eps_ln, eps_rms = (sb(n, [P, 1]) for n in ("neg_half", "eps_ln", "eps_rms"))
        causal = sb("causal", [P, P], BF16)
        head_row = sb("head_row", [P, NH, P], BF16)
        parity = sb("parity", [P, 2])
        expert_row = sb("expert_row", [P, EC, P], BF16)
        wa = sb("wa", [P, KC, 3, D])
        wo_a = sb("wo_a", [P, KC, D])
        wb = sb("wb", [P, KC, 5, D])
        wdn = sb("wdn", [P, KC, NE * BD + BD + NE])
        wup = sb("wup", [P, EC, D])
        wsu = sb("wsu", [P, D])
        vecs = sb("vecs", [P, 6 * KC + EC])
        g_col, b_col, nw_col = (vecs[:, i * KC:(i + 1) * KC] for i in range(3))
        bqkv = vecs[:, 3 * KC:6 * KC]
        bd_col = vecs[:, 6 * KC:]
        bfull = sb("bfull", [P, 3, KC])
        bq_par = sb("bq_par", [P, KC, 2])
        bsd_col = sb("bsd_col", [BD, 1])
        rows = sb("rows", [1, 2, D])
        bvb = sb("bvb", [P, KC, P])
        row_bc = sb("row_bc", [P, 2, D])
        mask_u8 = sb("mask_u8", [NB, P], U8)
        mask_f = sb("mask_f", [NB, P])
        valid = sb("valid", [P, NB])
        none_valid = sb("none_valid", [P, NB])
        key_cols = sb("key_cols", [P, NB, 3])

        x_in = [sb(f"x_in{i}", [P, D]) for i in range(2)]
        c_in = [sb(f"c_in{i}", [P, D]) for i in range(2)]
        x_bo = [sb(f"x_bo{i}", [P, D]) for i in range(2)]
        xn = sb("xn", [P, D])
        t1 = sb("t1", [P, 2, KC, P])
        t2 = sb("t2", [P, 2, KC, P])
        q_a, q_b = (sb(n, [P, KC, 2, P]) for n in ("q_a", "q_b"))
        k_a, k_b = (sb(n, [P, KC, P]) for n in ("k_a", "k_b"))
        v_a, v_b = (sb(n, [P, 8, 3, DH]) for n in ("v_a", "v_b"))
        den_a = sb("den_a", [P, 3, DH])
        den_b = [sb(f"den_b{i}", [P, 3, DH]) for i in range(2)]
        cols = [sb(f"cols{i}", [P, 3]) for i in range(2)]
        mdiag = [sb(f"mdiag{i}", [P, P], BF16) for i in range(2)]
        nm_a, nm_b = (sb(n, [P, NH], BF16) for n in ("nm_a", "nm_b"))
        nmt_a, nmt_b = (sb(n, [P, P], BF16) for n in ("nmt_a", "nmt_b"))
        e_a, e_b = (sb(n, [P, NR, 2, 2, P]) for n in ("e_a", "e_b"))
        rec_a, rec_b = (sb(n, [P, D]) for n in ("rec_a", "rec_b"))
        o_a, o_b = (sb(n, [P, KC, P]) for n in ("o_a", "o_b"))
        y_a, y_b, y_c = (sb(n, [P, D]) for n in ("y_a", "y_b", "y_c"))
        z_b = sb("z_b", [P, D])
        gate = sb("gate", [P, D])
        x1 = [sb(f"x1_{i}", [P, D]) for i in range(2)]
        xr = sb("xr", [P, D])
        x2 = sb("x2", [P, D])
        x2_b = sb("x2_b", [P, D])
        o_out = [sb(f"o_out{i}", [P, D]) for i in range(2)]
        st_x, st_a, st_b, st_c = (sb(n, [P, 6]) for n in ("st_x", "st_a", "st_b", "st_c"))
        mv_x, mv_a, mv_b, mv_c = (sb(n, [P, 2]) for n in ("mv_x", "mv_a", "mv_b", "mv_c"))
        ve_x, ve_a, ve_b, ve_c = (sb(n, [P, 1]) for n in ("ve_x", "ve_a", "ve_b", "ve_c"))
        rs_x, rs_a, rs_b, rs_c = (sb(n, [P, 1]) for n in ("rs_x", "rs_a", "rs_b", "rs_c"))
        rms = sb("rms", [P, 4])
        lg_t = sb("lg_t", [P, P])
        lg = sb("lg", [P, NE])
        rt = sb("rt", [P, 8, NE])
        rcol = sb("rcol", [P, 5])
        top8 = sb("top8", [P, 8])
        comb = sb("comb", [P, NE])
        comb3 = sb("comb3", [P, 3, NE], BF16)
        crest = sb("crest", [P, 2, NE])
        comb3_t = sb("comb3_t", [P, P], BF16)
        h = sb("h", [P, EC, P])
        hs = sb("hs", [P, P])
        hc = sb("hc", [P, EC, P])

        S = es.enter_context(nc.psum_tensor("S", [P, NR, 2, 2, P], F32))
        G = [es.enter_context(nc.psum_tensor(f"G{i}", [P, 512], F32)) for i in range(4)]

        w_in = sem("w_in")
        x_ld = [sem(f"x_ld{i}") for i in range(2)]
        c_ld = [sem(f"c_ld{i}") for i in range(2)]
        out_st = [sem(f"out_st{i}") for i in range(2)]
        k_pool, k_dve, k_pe, k_ready = sem("k_pool"), sem("k_dve"), sem("k_pe"), sem("k_ready")
        (xn_mv, xn_ve, xn_rs, xn_ok, xbo_ok, t1_mm, t1_sb, qka_mm, qka_sb, v_mm, v_sb, sma_mm, nma_ok,
         mta_mm, mta_sb, sta_mm, ea_ok, em_ok, oa_mm, oa_sb, woa_mm, ya_ok, mva_ok, vea_ok, rsa_ok,
         rm1, rm2, rm3, rma_ok, xr_ok) = (sem(n) for n in (
             "xn_mv xn_ve xn_rs xn_ok xbo_ok t1_mm t1_sb qka_mm qka_sb v_mm v_sb sma_mm nma_ok "
             "mta_mm mta_sb sta_mm ea_ok em_ok oa_mm oa_sb woa_mm ya_ok mva_ok vea_ok rsa_ok "
             "rm1 rm2 rm3 rma_ok xr_ok").split())
        (col_ok, bm_ok, tx_mm, tx_sb, qkb_mm, qkb_sb, gb_mm, gate_ok, smb_mm, nmb_ok, mtb_mm, mtb_sb,
         stb_mm, eb_ok, ob_mm, ob_sb, wob_mm, zb_ok, mvb_ok, veb_ok, rsb_ok, x2_ok, x2b_ok) = (
             sem(n) for n in (
                 "col_ok bm_ok tx_mm tx_sb qkb_mm qkb_sb gb_mm gate_ok smb_mm nmb_ok mtb_mm mtb_sb "
                 "stb_mm eb_ok ob_mm ob_sb wob_mm zb_ok mvb_ok veb_ok rsb_ok x2_ok x2b_ok").split())
        (ty_mm, ty_sb, dn2_mm, lgt_sb, dn1_mm, lt_mm, lg_ok, gap_ok, rth_ok, comb_ok, ct_mm, ct_sb,
         h_ok, ce_mm, hc_ok, up_mm, yc_ok, mvc_ok, vec_ok, rsc_ok, out_ok) = (sem(n) for n in (
             "ty_mm ty_sb dn2_mm lgt_sb dn1_mm lt_mm lg_ok gap_ok rth_ok comb_ok ct_mm ct_sb "
             "h_ok ce_mm hc_ok up_mm yc_ok mvc_ok vec_ok rsc_ok out_ok").split())

        def wait(eng, signal, n):
            if isinstance(n, int):
                n = min(n, NB)
                if n <= 0:
                    return
            eng.wait_ge(signal, n)

        def schedule(eng, step):
            for s in (0, 1):
                step(s, s % 2)
            with eng.Fori(2, NB - 3, 2) as i:
                step(i, 0)
                step(i + 1, 1)
            for s in range(NB - 2, NB + 2):
                step(s, s % 2)

        def live(s, lag):
            return not isinstance(s, int) or 0 <= s - lag < NB

        block = es.enter_context(nc.Block())

        @block.sync
        def _(sp):
            def load_x(b, p):
                sp.dma_start(x_in[p][:, :], x[bass.ds(b, 1), :, :].rearrange("a t d -> (a t) d")).then_inc(x_ld[p], 16)

            def load_c(b, p):
                sp.dma_start(c_in[p][:, :], ctx_in[bass.ds(b, 1), :, :].rearrange("a t d -> (a t) d")).then_inc(c_ld[p], 16)

            load_x(0, 0)
            sp.dma_start(vecs[:, :], cols_in).then_inc(w_in, 16)
            sp.dma_start(wa[:, :, :, :], wa_in).then_inc(w_in, 16)
            load_c(0, 0)
            load_x(1, 1)
            sp.dma_start(wdn[:, :, :], wdn_in).then_inc(w_in, 16)
            sp.dma_start(wup[:, :, :], wup_in).then_inc(w_in, 16)

            def step(s, p):
                if not isinstance(s, int) or s + 2 < NB:
                    wait(sp, xn_ok, s + 1)
                    wait(sp, xbo_ok, s + 1)
                    load_x(s + 2, p)
                if not isinstance(s, int) or s + 1 < NB:
                    sp.wait_ge(t1_mm, s + 1)
                    load_c(s + 1, 1 - p)
                if live(s, 2):
                    wait(sp, out_ok, s - 1)
                    sp.dma_start(out[bass.ds(s - 2, 1), :, :].rearrange("a t d -> (a t) d"),
                                 o_out[p][:, :]).then_inc(out_st[p], 16)

            schedule(sp, step)
            for p in range(2):
                sp.wait_ge(out_st[p], 16 * NB // 2)

        @block.gpsimd
        def _(pool):
            gp = nc.gpsimd
            gp.memset(identf[:, :], 0.0)
            gp.memset(ones[:, :], 1.0)
            gp.memset(onesb[:, :], 1.0)
            gp.memset(neg_half[:, :], -0.5)
            gp.memset(eps_ln[:, :], EPS_LN)
            gp.memset(eps_rms[:, :], EPS_RMS)
            gp.memset(causal[:, :], 0.0)
            gp.memset(head_row[:, :, :], 1.0)
            gp.memset(expert_row[:, :, :], 0.0)
            gp.memset(comb3_t[:, :], 0.0)
            gp.memset(hs[:, :], 0.0)
            gp.memset(den_a[:, :, :], 1.0)
            gp.memset(v_a[:, :, :, :], 0.0)
            gp.memset(v_b[:, :, :, :], 0.0)
            gp.memset(nmt_a[:, :], 0.0)
            gp.memset(nmt_b[:, :], 0.0)
            gp.memset(identb[:, :], 0.0).then_inc(k_pool, 1)
            pool.wait_ge(k_pool, 1)
            gp.affine_select(out=identf[:, :], in_=identf[:, :], compare_op=ALU.not_equal, fill=1.0,
                             base=0, pattern=[[-1, P]], channel_multiplier=1)
            gp.affine_select(out=identb[:, :], in_=identb[:, :], compare_op=ALU.not_equal, fill=1.0,
                             base=0, pattern=[[-1, P]], channel_multiplier=1)
            gp.affine_select(out=causal[:, :], in_=causal[:, :], compare_op=ALU.is_ge, fill=BIG,
                             base=0, pattern=[[-1, P]], channel_multiplier=1)
            gp.affine_select(out=head_row[:, :, :], in_=head_row[:, :, :], compare_op=ALU.is_equal, fill=0.0,
                             base=0, pattern=[[1, NH], [0, P]], channel_multiplier=-1)
            for part in range(3):
                if part:
                    pool.wait_ge(k_pool, 1 + part)
                last = gp.affine_select(out=expert_row[:, :, :].rearrange("e j (a b) -> e j a b", a=2),
                                        in_=expert_row[:, :, :].rearrange("e j (a b) -> e j a b", a=2),
                                        compare_op=ALU.not_equal, fill=0.5, base=NE * part,
                                        pattern=[[2, EC], [1, 2], [0, BD]], channel_multiplier=-1)
                last.then_inc(k_pool, 1)
            gp.memset(den_a[:, 1:2, :], 0.0)
            for i in range(2):
                gp.memset(den_b[i][:, :, :], 0.0)
            gp.memset(cols[0][:, :], 0.0).then_inc(k_pool, 1)
            pool.wait_ge(k_ready, 1)

            def rstd(ve, mv, rs, mv_ok, ve_ok, rs_ok, n, eps):
                wait(pool, mv_ok, n)
                gp.tensor_tensor(ve[:, :], mv[:, 1:2], eps, ALU.add).then_inc(ve_ok, 1)
                wait(pool, ve_ok, n)
                gp.tensor_tensor(rs[:, :], ve[:, :], neg_half[:, :], ALU.pow).then_inc(rs_ok, 1)

            def first(n, p):
                rstd(ve_x, mv_x, rs_x, xn_mv, xn_ve, xn_rs, n, eps_ln[:, :])
                wait(pool, ya_ok, n - 2)
                gp.tensor_tensor(x_bo[p][:, :], x_in[p][:, :], row_bc[:, 0, :], ALU.add).then_inc(xbo_ok, 1)

            first(1, 0)

            def step(s, p):
                if live(s, 0):
                    wait(pool, ob_mm, s - 1)
                    gp.tensor_copy(cols[p][:, :], key_cols[:, bass.ds(s, 1), :].rearrange("p a c -> p (a c)")).then_inc(col_ok, 1)
                    wait(pool, col_ok, s + 1)
                    gp.tensor_tensor(mdiag[p][:, :], identb[:, :], cols[p][:, 2:3].to_broadcast([P, P]), ALU.mult)
                    gp.tensor_scalar(den_b[p][:, 0::2, :], den_a[:, 0::2, :], cols[p][:, 1:2], None,
                                     ALU.mult).then_inc(bm_ok, 1)
                if live(s, 2):
                    rstd(ve_b, mv_b, rs_b, mvb_ok, veb_ok, rsb_ok, s - 1, eps_ln[:, :])
                if not isinstance(s, int) or s + 1 < NB:
                    first(s + 2, 1 - p)
                if live(s, 2):
                    wait(pool, x2_ok, s - 1)
                    wait(pool, yc_ok, s - 2)
                if live(s, 0):
                    wait(pool, ea_ok, s + 1)
                if live(s, 2):
                    gp.tensor_tensor(x2_b[:, :], x2[:, :], row_bc[:, 1, :], ALU.add).then_inc(x2b_ok, 1)
                if live(s, 0):
                    gp.affine_select(out=e_a[:, :, :, :, :].rearrange("p r c a q -> p (r c a) q"),
                                     in_=e_a[:, :, :, :, :].rearrange("p r c a q -> p (r c a) q"),
                                     compare_op=ALU.is_ge, fill=0.0, base=0, pattern=[[0, NH], [1, P]],
                                     channel_multiplier=-1).then_inc(em_ok, 1)
                if live(s, 2):
                    rstd(ve_c, mv_c, rs_c, mvc_ok, vec_ok, rsc_ok, s - 1, eps_ln[:, :])
                if live(s, 0):
                    rstd(ve_a, mv_a, rs_a, mva_ok, vea_ok, rsa_ok, s + 1, eps_ln[:, :])
                    wait(pool, rsa_ok, s + 1)
                    gp.tensor_tensor(rms[:, 0:1], mv_a[:, 1:2], rs_a[:, :], ALU.mult).then_inc(rm1, 1)
                    wait(pool, rm1, s + 1)
                    gp.tensor_tensor(rms[:, 1:2], rms[:, 0:1], rs_a[:, :], ALU.mult).then_inc(rm2, 1)
                    wait(pool, rm2, s + 1)
                    gp.tensor_tensor(rms[:, 2:3], rms[:, 1:2], eps_rms[:, :], ALU.add).then_inc(rm3, 1)
                    wait(pool, rm3, s + 1)
                    gp.tensor_tensor(rms[:, 3:4], rms[:, 2:3], neg_half[:, :], ALU.pow).then_inc(rma_ok, 1)

            schedule(pool, step)

        @block.scalar
        def _(act):
            ac = nc.scalar
            act.dma_start(mask_u8[:, :], mask).then_inc(w_in, 16)
            act.dma_start(rows[:, :, :], rows_in).then_inc(w_in, 16)
            act.dma_start(bsd_col[:, :], bsd_in).then_inc(w_in, 16)
            act.dma_start(wo_a[:, :, :], wo_a_in).then_inc(w_in, 16)
            act.dma_start(wb[:, :, :, :], wb_in).then_inc(w_in, 16)
            act.dma_start(wsu[:, :], wsu_in).then_inc(w_in, 16)
            act.wait_ge(w_in, 16 * WEIGHTS)

            def first_t(s):
                act.wait_ge(t1_mm, s + 1)
                if live(s, 0) and live(s, 1):
                    ac.activation(t1[:, :, :, :].rearrange("p a k t -> p (a k t)"), G[2][:, :], ACT.Copy).then_inc(t1_sb, 1)
                elif live(s, 0):
                    ac.activation(t1[:, 0, :, :].rearrange("p k t -> p (k t)"), G[2][:, 0:256], ACT.Copy).then_inc(t1_sb, 1)
                else:
                    ac.activation(t1[:, 1, :, :].rearrange("p k t -> p (k t)"), G[2][:, 256:512], ACT.Copy).then_inc(t1_sb, 1)

            first_t(0)

            def step(s, p):
                A, B, B2 = live(s, 0), live(s, 1), live(s, 2)
                if B:
                    wait(act, tx_mm, s)
                    wait(act, gb_mm, s - 1)
                    ac.activation(t2[:, 0, :, :].rearrange("p k t -> p (k t)"), G[2][:, 0:256], ACT.Copy).then_inc(tx_sb, 1)
                if A or B:
                    act.wait_ge(v_mm, s + 1)
                if A:
                    wait(act, oa_mm, s)
                    last = ac.activation(v_a[:, :, 0::2, :], G[1][:, 0:256].rearrange("p (a b d) -> p a b d", b=2, d=DH), ACT.Copy)
                if B:
                    wait(act, bm_ok, s)
                    wait(act, ob_mm, s - 1)
                    last = ac.activation(v_b[:, :, 0::2, :], G[1][:, 256:512].rearrange("p (a b d) -> p a b d", b=2, d=DH),
                                         ACT.Copy, scale=cols[1 - p][:, 0:1])
                if A or B:
                    last.then_inc(v_sb, 1)
                if B2:
                    wait(act, ty_mm, s - 1)
                    wait(act, dn2_mm, s - 2)
                    ac.activation(t2[:, 1, :, :].rearrange("p k t -> p (k t)"), G[2][:, 0:256], ACT.Copy).then_inc(ty_sb, 1)
                if A:
                    wait(act, mta_mm, s + 1)
                    wait(act, sta_mm, s)
                    ac.activation(nmt_a[0:NH, :], G[2][0:NH, 0:64].bitcast(BF16), ACT.Copy).then_inc(mta_sb, 1)
                if B2:
                    wait(act, dn2_mm, s - 1)
                    wait(act, lt_mm, s - 2)
                    ac.activation(lg_t[BD:BD + NE, :], G[1][BD:BD + NE, 0:P], ACT.Copy).then_inc(lgt_sb, 1)
                    wait(act, up_mm, s - 2)
                    wait(act, hc_ok, s - 2)
                    ac.activation(hs[0:BD, :], G[1][0:BD, 0:P], ACT.Gelu, bias=bsd_col[:, :])
                    wait(act, dn1_mm, s - 1)
                    for j in range(EC):
                        last = ac.activation(h[:, j, :], G[0][:, j * P:(j + 1) * P], ACT.Gelu, bias=bd_col[:, j:j + 1])
                    last.then_inc(h_ok, 1)
                    wait(act, gap_ok, s - 1)
                    ac.activation(rcol[:, 3:4], rcol[:, 2:3], ACT.Tanh, scale=0.5).then_inc(rth_ok, 1)
                if A:
                    wait(act, sta_mm, s + 1)
                    wait(act, oa_mm, s)
                    ac.activation(e_a[:, :, :, :, :].rearrange("p r c a q -> p (r c a q)"),
                                  S[:, :, :, :, :].rearrange("p r c a q -> p (r c a q)"), ACT.Exp,
                                  scale=SCALE).then_inc(ea_ok, 1)
                if B:
                    wait(act, gb_mm, s)
                    wait(act, zb_ok, s - 1)
                    ac.activation(gate[:, :], G[3][:, 0:256], ACT.Tanh, scale=0.5).then_inc(gate_ok, 1)
                if live(s + 1, 0) or live(s + 1, 1):
                    first_t(s + 1)
                if B:
                    wait(act, mtb_mm, s)
                    wait(act, stb_mm, s - 1)
                    ac.activation(nmt_b[0:NH, :], G[2][0:NH, 0:64].bitcast(BF16), ACT.Copy).then_inc(mtb_sb, 1)
                    wait(act, stb_mm, s)
                    wait(act, ob_mm, s - 1)
                    ac.activation(e_b[:, :, :, :, :].rearrange("p r c a q -> p (r c a q)"),
                                  S[:, :, :, :, :].rearrange("p r c a q -> p (r c a q)"), ACT.Exp,
                                  scale=SCALE, bias=cols[1 - p][:, 2:3]).then_inc(eb_ok, 1)

            schedule(act, step)

        @block.vector
        def _(dve):
            v = nc.vector
            chain = [0]

            def link(ins):
                chain[0] += 1
                ins.then_inc(k_dve, 1)
                dve.wait_ge(k_dve, chain[0])

            dve.wait_ge(w_in, 16 * WEIGHTS)
            dve.wait_ge(k_pool, 5)
            v.reduce_sum(parity[:, :], identf[:, :].rearrange("p (r a d) -> p a r d", a=2, d=DH), axis=AX.XY)
            link(v.tensor_copy(mask_f[:, :], mask_u8[:, :]))
            dve.wait_ge(k_pe, 1)
            v.tensor_copy(valid[:, :], G[0][:, 0:NB])
            link(v.tensor_tensor(bfull[:, :, :].rearrange("p a k -> p (a k)"), G[1][:, 0:6],
                                 bqkv, ALU.add))
            for k in range(KC):
                v.tensor_scalar(bq_par[:, k, :], parity[:, :], bfull[:, 0, k:k + 1], None, ALU.mult)
                v.tensor_scalar(bvb[:, k, :], ones[:, :], bfull[:, 2, k:k + 1], None, ALU.mult)
                v.tensor_scalar(wa[:, k, :, :].rearrange("p a n -> p (a n)"), wa[:, k, :, :].rearrange("p a n -> p (a n)"),
                                g_col[:, k:k + 1], None, ALU.mult)
                v.tensor_scalar(wb[:, k, 0:2, :].rearrange("p a n -> p (a n)"), wb[:, k, 0:2, :].rearrange("p a n -> p (a n)"),
                                nw_col[:, k:k + 1], None, ALU.mult)
                v.tensor_scalar(wb[:, k, 4, :], wb[:, k, 4, :], 0.5, None, ALU.mult)
            v.tensor_scalar(wsu[BD:BD + NE, :], wsu[BD:BD + NE, :], 0.5, None, ALU.mult)
            link(v.tensor_copy(key_cols[:, :, 0], valid[:, :]))
            dve.wait_ge(k_pe, 2)
            link(v.tensor_scalar(none_valid[:, :], G[2][:, 0:NB], 0.5, None, ALU.is_lt))
            link(v.tensor_tensor(key_cols[:, :, 1], none_valid[:, :], valid[:, :], ALU.max))
            v.tensor_scalar(key_cols[:, :, 2], key_cols[:, :, 1], -BIG, BIG, ALU.mult, ALU.add)
            v.tensor_copy(row_bc[:, :, :].rearrange("p a n -> p (a n)"), G[3][:, :]).then_inc(k_ready, 1)

            def stats(y, st, mv, mv_ok):
                v.bn_stats(st[:, :], y)
                dve.drain()
                v.bn_aggr(mv[:, :], st[:, :]).then_inc(mv_ok, 1)

            def first_norm(n, p, loaded):
                dve.wait_ge(x_ld[p], loaded)
                stats(x_in[p][:, :], st_x, mv_x, xn_mv)
                wait(dve, xn_rs, n)
                if not isinstance(n, int) or n > 1:
                    dve.wait_ge(t1_mm, n - 1)
                v.tensor_scalar(xn[:, :], x_in[p][:, :], mv_x[:, 0:1], rs_x[:, :], ALU.subtract, ALU.mult).then_inc(xn_ok, 1)

            first_norm(1, 0, 16)

            def router(n):
                wait(dve, lt_mm, n)
                v.tensor_copy(lg[:, :], G[2][:, 0:NE]).then_inc(lg_ok, 1)
                for i in range(2):
                    score = lg[:, :] if i == 0 else rt[:, 3, :]
                    equal, count, first = rt[:, 0, :], rt[:, 1, :], rt[:, 4 + i, :]
                    dve.drain()
                    v.reduce_max(rcol[:, i:i + 1], score, axis=AX.X)
                    dve.drain()
                    v.tensor_scalar(equal, score, rcol[:, i:i + 1], None, ALU.is_equal)
                    dve.drain()
                    v.tensor_tensor_scan(count, ones[:, 0:NE], equal, 0.0, ALU.mult, ALU.add)
                    dve.drain()
                    v.scalar_tensor_tensor(out=first, in0=count, scalar=1.0, in1=equal, op0=ALU.is_equal, op1=ALU.mult)
                    if i == 0:
                        dve.drain()
                        v.scalar_tensor_tensor(out=rt[:, 3, :], in0=first, scalar=3.0 * BIG, in1=lg[:, :],
                                               op0=ALU.mult, op1=ALU.add)
                v.tensor_tensor(rcol[:, 2:3], rcol[:, 0:1], rcol[:, 1:2], ALU.subtract).then_inc(gap_ok, 1)
                dve.drain()
                v.tensor_tensor(rt[:, 6, :], rt[:, 4, :], rt[:, 5, :], ALU.add)
                v.tensor_tensor(rt[:, 7, :], rt[:, 4, :], rt[:, 5, :], ALU.subtract)
                dve.drain()
                wait(dve, rth_ok, n)
                v.scalar_tensor_tensor(out=comb[:, :], in0=rt[:, 7, :], scalar=rcol[:, 3:4], in1=rt[:, 6, :],
                                       op0=ALU.mult, op1=ALU.add)
                dve.drain()
                v.tensor_copy(comb3[:, 0, :], comb[:, :])
                dve.drain()
                v.tensor_tensor(crest[:, 0, :], comb[:, :], comb3[:, 0, :], ALU.subtract)
                dve.drain()
                v.tensor_copy(comb3[:, 1, :], crest[:, 0, :])
                dve.drain()
                v.tensor_tensor(comb3[:, 2, :], crest[:, 0, :], comb3[:, 1, :], ALU.subtract).then_inc(comb_ok, 1)

            def step(s, p):
                A, B, B2 = live(s, 0), live(s, 1), live(s, 2)
                if A:
                    wait(dve, qka_mm, s + 1)
                    wait(dve, sta_mm, s)
                    for c in range(KC):
                        for a in range(2):
                            v.tensor_scalar(q_a[:, c, a, :], G[1][:, c * P:(c + 1) * P], parity[:, a:a + 1],
                                            bq_par[:, c, a:a + 1], ALU.mult, ALU.add)
                        last = v.tensor_scalar(k_a[:, c, :], G[1][:, 256 + c * P:256 + (c + 1) * P],
                                               bfull[:, 1, c:c + 1], None, ALU.add)
                    last.then_inc(qka_sb, 1)
                if B2:
                    wait(dve, ob_mm, s - 1)
                    v.reciprocal(rec_b[:, :], G[3][:, 256:512])
                    dve.drain()
                    wait(dve, wob_mm, s - 2)
                    v.tensor_tensor(o_b[:, :, :].rearrange("p c t -> p (c t)"), G[3][:, 0:256], rec_b[:, :], ALU.mult).then_inc(ob_sb, 1)
                    wait(dve, wob_mm, s - 1)
                    v.scalar_tensor_tensor(out=z_b[:, :], in0=gate[:, :], scalar=1.0, in1=G[0][:, 0:256],
                                           op0=ALU.add, op1=ALU.mult).then_inc(zb_ok, 1)
                    dve.drain()
                    v.tensor_tensor(y_b[:, :], z_b[:, :], x1[p][:, :], ALU.add)
                    dve.drain()
                    stats(y_b[:, :], st_b, mv_b, mvb_ok)
                    wait(dve, rsb_ok, s - 1)
                    wait(dve, ty_mm, s - 2)
                    wait(dve, x2b_ok, s - 2)
                    v.tensor_scalar(x2[:, :], y_b[:, :], mv_b[:, 0:1], rs_b[:, :], ALU.subtract, ALU.mult).then_inc(x2_ok, 1)
                if A:
                    wait(dve, sma_mm, s + 1)
                    v.tensor_reduce(nm_a[:, :], S[:, :, :, :, :].rearrange("p r c a k -> p (r c a) k"),
                                    op=ALU.max, axis=AX.X, negate=True).then_inc(nma_ok, 1)
                if B:
                    wait(dve, qkb_mm, s)
                    wait(dve, stb_mm, s - 1)
                    for a in range(2):
                        v.tensor_scalar(q_b[:, :, a, :], G[3][:, 0:256].rearrange("p (c t) -> p c t", c=KC),
                                        parity[:, a:a + 1], None, ALU.mult)
                    v.tensor_copy(k_b[:, :, :].rearrange("p c t -> p (c t)"), G[3][:, 256:512]).then_inc(qkb_sb, 1)
                if not isinstance(s, int) or s + 1 < NB:
                    first_norm(s + 2, 1 - p, 8 * (s + 1) + 16 - 8 * (1 - p))
                if B2:
                    router(s - 1)
                    wait(dve, ct_mm, s - 1)
                    wait(dve, up_mm, s - 2)
                    v.tensor_copy(comb3_t[0:3 * NE, :], G[2][0:3 * NE, 0:64].bitcast(BF16))
                    v.tensor_copy(hs[BD:BD + NE, :], G[2][0:NE, 64:192]).then_inc(ct_sb, 1)
                    wait(dve, ce_mm, s - 1)
                    wait(dve, h_ok, s - 1)
                    v.tensor_tensor(hc[:, :, :].rearrange("p j t -> p (j t)"), h[:, :, :].rearrange("p j t -> p (j t)"),
                                    G[0][:, :], ALU.mult).then_inc(hc_ok, 1)
                if B:
                    wait(dve, smb_mm, s)
                    v.tensor_reduce(nm_b[:, :], S[:, :, :, :, :].rearrange("p r c a k -> p (r c a) k"),
                                    op=ALU.max, axis=AX.X, negate=True).then_inc(nmb_ok, 1)
                if B2:
                    wait(dve, up_mm, s - 1)
                    wait(dve, x2b_ok, s - 1)
                    v.tensor_tensor(y_c[:, :], G[3][:, 0:256], x2_b[:, :], ALU.add).then_inc(yc_ok, 1)
                    dve.drain()
                    stats(y_c[:, :], st_c, mv_c, mvc_ok)
                if A:
                    wait(dve, oa_mm, s + 1)
                    v.reciprocal(rec_a[:, :], G[1][:, 256:512])
                    dve.drain()
                    v.tensor_tensor(o_a[:, :, :].rearrange("p c t -> p (c t)"), G[1][:, 0:256], rec_a[:, :], ALU.mult).then_inc(oa_sb, 1)
                if B2:
                    wait(dve, rsc_ok, s - 1)
                    if not isinstance(s, int) or s >= 4:
                        dve.wait_ge(out_st[p], 8 * s - 16 - 8 * p)
                    v.tensor_scalar(o_out[p][:, :], y_c[:, :], mv_c[:, 0:1], rs_c[:, :], ALU.subtract, ALU.mult).then_inc(out_ok, 1)
                if A:
                    wait(dve, woa_mm, s + 1)
                    wait(dve, xbo_ok, s + 1)
                    v.tensor_tensor(y_a[:, :], G[0][:, 0:256], x_bo[p][:, :], ALU.add).then_inc(ya_ok, 1)
                    dve.drain()
                    stats(y_a[:, :], st_a, mv_a, mva_ok)
                    wait(dve, rsa_ok, s + 1)
                    v.tensor_scalar(x1[p][:, :], y_a[:, :], mv_a[:, 0:1], rs_a[:, :], ALU.subtract, ALU.mult)
                    dve.drain()
                    wait(dve, rma_ok, s + 1)
                    wait(dve, tx_mm, s)
                    v.tensor_scalar(xr[:, :], x1[p][:, :], rms[:, 3:4], None, ALU.mult).then_inc(xr_ok, 1)

            schedule(dve, step)

        @block.tensor
        def _(pe):
            mm = nc.tensor.matmul

            pe.wait_ge(k_pool, 5)
            pe.wait_ge(w_in, 16 * WEIGHTS)
            pe.wait_ge(k_dve, 1)
            nc.tensor.transpose(G[0][:, 0:NB], mask_f[:, :], identf[0:NB, 0:NB])
            for i in range(3):
                for m in range(KC):
                    for k in range(KC):
                        last = mm(G[1][:, i * KC + m:i * KC + m + 1], wa[:, k, i, m * P:(m + 1) * P], b_col[:, k:k + 1],
                                  start=(k == 0), stop=(k == KC - 1))
            last.then_inc(k_pe, 1)
            pe.wait_ge(k_dve, 3)
            mm(G[2][:, 0:NB], ones[:, :], valid[:, :], start=True, stop=True)
            mm(G[3][:, 0:D], ones[0:1, :], rows[:, 0, :], start=True, stop=False)
            for k in range(KC):
                mm(G[3][:, 0:D], bvb[:, k, :], wo_a[:, k, :], start=False, stop=(k == KC - 1))
            mm(G[3][:, D:2 * D], ones[0:1, :], rows[:, 1, :], start=True, stop=True).then_inc(k_pe, 1)
            pe.wait_ge(k_ready, 1)

            def project_t(dst, w, i, src, a):
                for m in range(KC):
                    for k in range(KC):
                        last = mm(dst[:, m * P:(m + 1) * P], w[:, k, i, m * P:(m + 1) * P], src[:, a, k, :],
                                  start=(k == 0), stop=(k == KC - 1))
                return last

            def project(dst, src, w, i):
                for k in range(KC):
                    last = mm(dst, src[:, k, :], w[:, k, i, :], start=(k == 0), stop=(k == KC - 1))
                return last

            def high(t):
                return t.bitcast(BF16)

            def scores_for_max(q, k, mask_l, mask_r):
                for r in range(NR):
                    mm(S[:, r, :, :, :].rearrange("p c a k -> p (c a) k"), mask_l,
                       mask_r.unsqueeze(1).to_broadcast([P, 4, P]), start=True, stop=False, skip_group_check=True)
                for c in range(KC):
                    for a in range(2):
                        for r in range(NR):
                            g = slice(32 * r, 32 * r + 32)
                            last = mm(S[:, r, c, a, :], high(q[g, c, a, :])[:, 1::2], high(k[g, c, :])[:, 1::2],
                                      start=False, stop=True, skip_group_check=True)
                return last

            def scores_t(q, k, nmt):
                for r in range(NR):
                    for c in range(KC):
                        for a in range(2):
                            mm(S[:, r, c, a, :], head_row[:, 4 * r + 2 * c + a, :], nmt[:, :],
                               start=(c == 0 and a == 0), stop=False, skip_group_check=True)
                for c in range(KC):
                    for r in range(NR):
                        g = slice(32 * r, 32 * r + 32)
                        last = mm(S[:, r, c, :, :], k[g, c, :], q[g, c, :, :], start=False, stop=True,
                                  skip_group_check=True)
                return last

            def values(dst, v_, e, den):
                for c in range(KC):
                    for a in range(2):
                        for r in range(NR):
                            mm(dst[32 * r:32 * r + 32, c * P:(c + 1) * P],
                               v_[:, 4 * c + r, a:a + 2, :].rearrange("p a d -> p (a d)"), e[:, r, c, a, :],
                               start=(a == 0), stop=(a == 1))
                for a in range(2):
                    for r in range(NR):
                        last = mm(dst[32 * r:32 * r + 32, 256:512].rearrange("p (c q) -> p c q", c=KC),
                                  den[:, a:a + 2, :].rearrange("p a d -> p (a d)"), e[:, r, :, a, :],
                                  start=(a == 0), stop=(a == 1))
                return last

            def turn(dst, src):
                for k in range(KC):
                    last = nc.tensor.transpose(dst[:, k * P:(k + 1) * P], src[:, k * P:(k + 1) * P], identf[:, :])
                return last

            def first_t(s, p):
                if live(s, 0):
                    wait(pe, xn_ok, s + 1)
                    last = turn(G[2][:, 0:256], xn)
                if live(s, 1):
                    pe.wait_ge(c_ld[1 - p], 8 * (s - 1) + 16 - 8 * (1 - p))
                    last = turn(G[2][:, 256:512], c_in[1 - p])
                last.then_inc(t1_mm, 1)

            first_t(0, 0)

            def step(s, p):
                A, B, B2 = live(s, 0), live(s, 1), live(s, 2)
                if A or B:
                    pe.wait_ge(t1_sb, s + 1)
                if A:
                    wait(pe, oa_sb, s)
                    project_t(G[1][:, 0:256], wa, 0, t1, 0)
                    project_t(G[1][:, 256:512], wa, 1, t1, 0).then_inc(qka_mm, 1)
                if B2:
                    wait(pe, eb_ok, s - 1)
                    wait(pe, yc_ok, s - 2)
                    wait(pe, qkb_sb, s - 1)
                    values(G[3], v_b, e_b, den_b[p]).then_inc(ob_mm, 1)
                if B:
                    wait(pe, mtb_sb, s - 1)
                    wait(pe, xr_ok, s)
                    turn(G[2][:, 0:256], xr).then_inc(tx_mm, 1)
                if A or B:
                    wait(pe, qka_sb, s + 1)
                if A:
                    last = project(G[1][:, 0:256], t1[:, 0, :, :], wa, 2)
                if B:
                    last = project(G[1][:, 256:512], t1[:, 1, :, :], wb, 3)
                if A or B:
                    last.then_inc(v_mm, 1)
                if B2:
                    wait(pe, ob_sb, s - 1)
                    wait(pe, ya_ok, s)
                    project(G[0][:, 0:256], o_b, wb, 4).then_inc(wob_mm, 1)
                if A:
                    wait(pe, qka_sb, s + 1)
                    wait(pe, eb_ok, s - 1)
                    scores_for_max(q_a, k_a, identb[:, :], causal[:, :]).then_inc(sma_mm, 1)
                if B:
                    wait(pe, ob_sb, s - 1)
                    project_t(G[3][:, 256:512], wb, 2, t1, 1)
                if B2:
                    wait(pe, x2_ok, s - 1)
                    wait(pe, tx_sb, s)
                    turn(G[2][:, 0:256], x2).then_inc(ty_mm, 1)
                if B:
                    wait(pe, tx_sb, s)
                    project_t(G[3][:, 0:256], wb, 0, t2, 0).then_inc(qkb_mm, 1)
                if B2:
                    wait(pe, ty_sb, s - 1)
                    wait(pe, zb_ok, s - 1)
                    for j in range(EC):
                        for k in range(KC):
                            last = mm(G[0][:, j * P:(j + 1) * P], wdn[:, k, j * P:(j + 1) * P], t2[:, 1, k, :],
                                      start=(k == 0), stop=(k == KC - 1))
                    last.then_inc(dn1_mm, 1)
                if A:
                    wait(pe, nma_ok, s + 1)
                    wait(pe, tx_sb, s)
                    wait(pe, ty_sb, s - 1)
                    nc.tensor.transpose(G[2][0:NH, 0:64].bitcast(BF16), nm_a[:, :], identb[:, :]).then_inc(mta_mm, 1)
                if B2:
                    pe.wait_ge(v_sb, min(s + 1, NB + 1) if isinstance(s, int) else s + 1)
                    for k in range(KC):
                        last = mm(G[1][0:BD + NE, 0:P], wdn[:, k, NE * BD:], t2[:, 1, k, :], start=(k == 0), stop=(k == KC - 1))
                    last.then_inc(dn2_mm, 1)
                if A:
                    wait(pe, mta_sb, s + 1)
                if B2:
                    wait(pe, mta_sb, s + 1)
                    wait(pe, lgt_sb, s - 1)
                    mm(G[2][:, 0:NE], lg_t[BD:BD + NE, :], identf[BD:BD + NE, BD:BD + NE], start=True, stop=True).then_inc(lt_mm, 1)
                if A:
                    scores_t(q_a, k_a, nmt_a).then_inc(sta_mm, 1)
                if B2:
                    wait(pe, comb_ok, s - 1)
                    wait(pe, lg_ok, s - 1)
                    nc.tensor.transpose(G[2][0:NE, 64:192], comb[:, :], identf[:, :])
                    nc.tensor.transpose(G[2][0:3 * NE, 0:64].bitcast(BF16), comb3[:, :, :].rearrange("p a e -> p (a e)"),
                                        identb[:, :]).then_inc(ct_mm, 1)
                if B:
                    wait(pe, qkb_sb, s)
                    project(G[3][:, 0:256], t2[:, 0, :, :], wb, 1).then_inc(gb_mm, 1)
                if B2:
                    wait(pe, ct_sb, s - 1)
                    wait(pe, h_ok, s - 1)
                    for j in range(EC):
                        last = mm(G[0][:, j * P:(j + 1) * P], expert_row[:, j, :], comb3_t[:, :], start=True, stop=True)
                    last.then_inc(ce_mm, 1)
                if live(s + 1, 0) or live(s + 1, 1):
                    wait(pe, ct_sb, s - 1)
                    wait(pe, mta_sb, s + 1)
                    first_t(s + 1, 1 - p)
                if B:
                    wait(pe, ea_ok, s + 1)
                    wait(pe, bm_ok, s)
                    scores_for_max(q_b, k_b, onesb[:, :], mdiag[1 - p][:, :]).then_inc(smb_mm, 1)
                if B2:
                    wait(pe, gate_ok, s)
                    wait(pe, hc_ok, s - 1)
                    mm(G[3][:, 0:256], hs[:, :], wsu[:, :], start=True, stop=False)
                    for j in range(EC):
                        last = mm(G[3][:, 0:256], hc[:, j, :], wup[:, j, :], start=False, stop=(j == EC - 1))
                    last.then_inc(up_mm, 1)
                if B:
                    wait(pe, nmb_ok, s)
                    pe.wait_ge(t1_sb, min(s + 2, NB + 1) if isinstance(s, int) else s + 2)
                    nc.tensor.transpose(G[2][0:NH, 0:64].bitcast(BF16), nm_b[:, :], identb[:, :]).then_inc(mtb_mm, 1)
                if A:
                    wait(pe, em_ok, s + 1)
                    wait(pe, v_sb, s + 1)
                    wait(pe, h_ok, s - 1)
                    values(G[1], v_a, e_a, den_a).then_inc(oa_mm, 1)
                if B:
                    wait(pe, mtb_sb, s)
                    scores_t(q_b, k_b, nmt_b).then_inc(stb_mm, 1)
                if A:
                    wait(pe, oa_sb, s + 1)
                    wait(pe, hc_ok, s - 1)
                    for k in range(KC):
                        last = mm(G[0][:, 0:256], o_a[:, k, :], wo_a[:, k, :], start=(k == 0), stop=(k == KC - 1))
                    last.then_inc(woa_mm, 1)

            schedule(pe, step)


_OUT = ((NB, P, D), "float32")


def kernel(x, ctx_2048, mask_BxS2_bk0, L0_attn_ln_g, L0_attn_ln_b, L0_attn_Wq, L0_attn_bq, L0_attn_Wk,
           L0_attn_bk, L0_attn_Wv, L0_attn_bv, L0_attn_Wo, L0_attn_bo, L0_xattn_norm_w, L0_xattn_wq,
           L0_xattn_wk, L0_xattn_wv, L0_xattn_wo, L0_xattn_wg, L0_ffn_gate_w, L0_ffn_wd, L0_ffn_bd,
           L0_ffn_wu, L0_ffn_bu, L0_ffn_ws_d, L0_ffn_bs_d, L0_ffn_ws_u, L0_ffn_bs_u):
    import numpy as np
    import concourse.bacc as bacc
    from concourse.bass_utils import run_bass_kernel_spmd

    A = np.asarray

    def k_rows(*ws):
        w = np.concatenate(ws, axis=1)
        return w.reshape(-1, P, w.shape[1]).transpose(1, 0, 2)

    def columns(*vs):
        return np.concatenate([A(v).reshape(-1, P) for v in vs]).T

    wd, wu = A(L0_ffn_wd), A(L0_ffn_wu)
    laid_out = [
        ("x", A(x)), ("ctx", A(ctx_2048)), ("mask", A(mask_BxS2_bk0)),
        ("vectors", columns(L0_attn_ln_g, L0_attn_ln_b, L0_xattn_norm_w, L0_attn_bq, L0_attn_bk, L0_attn_bv,
                            L0_ffn_bd)),
        ("rows", np.stack([A(L0_attn_bo), A(L0_ffn_bs_u)])[None]),
        ("wa", k_rows(A(L0_attn_Wq), A(L0_attn_Wk), A(L0_attn_Wv)).reshape(P, KC, 3, D)),
        ("wo_a", k_rows(A(L0_attn_Wo))),
        ("wb", k_rows(A(L0_xattn_wq).T, A(L0_xattn_wg).T, A(L0_xattn_wk).T, A(L0_xattn_wv).T,
                      A(L0_xattn_wo).T).reshape(P, KC, 5, D)),
        ("wdn", k_rows(wd.reshape(-1, D).T, A(L0_ffn_ws_d).T, A(L0_ffn_gate_w).T)),
        ("wup", k_rows(wu.transpose(0, 2, 1).reshape(-1, D))),
        ("wsu", np.concatenate([A(L0_ffn_ws_u).T, A(L0_ffn_bu), np.zeros((P - BD - NE, D), np.float32)])),
        ("bsd", A(L0_ffn_bs_d)[:, None]),
    ]
    nc = bacc.Bacc("TRN2", target_bir_lowering=False, num_devices=1)
    arrays, args = {}, []
    for name, a in laid_out:
        a = np.ascontiguousarray(a)
        arrays[f"in_{name}"] = a
        args.append(nc.dram_tensor(f"in_{name}", a.shape, mybir.dt.from_np(a.dtype), kind="ExternalInput").ap())
    out = nc.dram_tensor("out", _OUT[0], mybir.dt.from_np(np.dtype(_OUT[1])), kind="ExternalOutput").ap()
    decoder_layer(nc, *args, out)
    r = run_bass_kernel_spmd(nc, [arrays], core_ids=[0])
    return r.results[0]["out"]
```

```python
import concourse.bass as bass
from concourse import mybir
from contextlib import ExitStack

F32 = mybir.dt.float32
BF16 = mybir.dt.bfloat16
U8 = mybir.dt.uint8
ALU = mybir.AluOpType
ACT = mybir.ActivationFunctionType
AX = mybir.AxisListType

NB = 16
P = 128
D = 256
KC = D // P
NH = 16
DH = D // NH
NR = 4
NE = 8
BD = 64
EC = NE * BD // P
SCALE = DH ** -0.5
BIG = -1.0e30
EPS_LN = 1e-5
EPS_RMS = 1e-6


def decoder_layer(nc, x, ctx_in, mask, cols_in, rows_in, wa_in, wo_a_in, wb_in, wdn_in, wup_in, wsu_in,
                  bsd_in, out):
    es = ExitStack()
    with es:
        def sb(name, shape, dt=F32):
            return es.enter_context(nc.sbuf_tensor(name, shape, dt))

        def sem(name):
            return es.enter_context(nc.semaphore(name))

        identf = sb("identf", [P, P])
        identb = sb("identb", [P, P], BF16)
        ones = sb("ones", [P, P])
        neg_half = sb("neg_half", [P, 2])
        causal = sb("causal", [P, P], BF16)
        head_row = sb("head_row", [P, NH, P], BF16)
        parity = sb("parity", [P, 2])
        other = sb("other", [P, 2])
        expert_row = sb("expert_row", [P, EC, P], BF16)
        wa = sb("wa", [P, KC, 3, D])
        wo_a = sb("wo_a", [P, KC, D])
        wb = sb("wb", [P, KC, 5, D])
        wdn = sb("wdn", [P, KC, NE * BD + BD + NE])
        wup = sb("wup", [P, EC, D])
        wsu = sb("wsu", [P, D])
        vecs = sb("vecs", [P, 6 * KC + EC])
        g_col, b_col, nw_col = (vecs[:, i * KC:(i + 1) * KC] for i in range(3))
        bq_col, bk_col, bv_col = (vecs[:, i * KC:(i + 1) * KC] for i in range(3, 6))
        bd_col = vecs[:, 6 * KC:]
        bq_par = sb("bq_par", [P, KC, 2])
        bsd_col = sb("bsd_col", [BD, 1])
        rows = sb("rows", [1, 2, D])
        bvb = sb("bvb", [P, KC, P])
        row_bc = sb("row_bc", [P, 2, D])
        mask_u8 = sb("mask_u8", [NB, P], U8)
        mask_f = sb("mask_f", [NB, P])
        mask_g = sb("mask_g", [NB, P])
        mask_any = sb("mask_any", [NB, 2])
        mask_add = sb("mask_add", [P, P], BF16)
        valid = sb("valid", [P, NB])
        none_valid = sb("none_valid", [P, NB])
        key_cols = sb("key_cols", [P, NB, 3])

        x_in = [sb(f"x_in{i}", [P, D]) for i in range(2)]
        c_t = [sb(f"c_t{i}", [P, KC, P]) for i in range(2)]
        x_bo = [sb(f"x_bo{i}", [P, D]) for i in range(2)]
        xn = sb("xn", [P, D])
        t1 = sb("t1", [P, KC, P])
        t2 = sb("t2", [P, 2, KC, P])
        q_a, q_b = (sb(n, [P, KC, 2, P]) for n in ("q_a", "q_b"))
        k_a, k_b = (sb(n, [P, KC, P]) for n in ("k_a", "k_b"))
        v_a = sb("v_a", [P, 8, 3, DH])
        v_b = [sb(f"v_b{i}", [P, 8, 3, DH]) for i in range(2)]
        den_a = sb("den_a", [P, 3, DH])
        den_b = [sb(f"den_b{i}", [P, 3, DH]) for i in range(2)]
        cols = [sb(f"cols{i}", [P, 3]) for i in range(2)]
        mask_t = [sb(f"mask_t{i}", [P, 2, P]) for i in range(2)]
        q_m = sb("q_m", [P, 2, KC, P], BF16)
        k_m = sb("k_m", [P, 2, KC, P], BF16)
        nm_a, nm_b = (sb(n, [P, NH], BF16) for n in ("nm_a", "nm_b"))
        nmt_a, nmt_b = (sb(n, [P, P], BF16) for n in ("nmt_a", "nmt_b"))
        e_a, e_b = (sb(n, [P, NR, 2, 2, P]) for n in ("e_a", "e_b"))
        rec_a, rec_b = (sb(n, [P, D]) for n in ("rec_a", "rec_b"))
        o_a, o_b = (sb(n, [P, KC, P]) for n in ("o_a", "o_b"))
        y_a, y_b, y_c = (sb(n, [P, D]) for n in ("y_a", "y_b", "y_c"))
        z_b = sb("z_b", [P, D])
        gate = sb("gate", [P, D])
        x1 = [sb(f"x1_{i}", [P, D]) for i in range(2)]
        xr = sb("xr", [P, D])
        x2 = sb("x2", [P, D])
        x2_b = sb("x2_b", [P, D])
        o_out = [sb(f"o_out{i}", [P, D]) for i in range(2)]
        st_x, st_a, st_b, st_c = (sb(n, [P, 6]) for n in ("st_x", "st_a", "st_b", "st_c"))
        mv_x, mv_a, mv_b, mv_c = (sb(n, [P, 2]) for n in ("mv_x", "mv_a", "mv_b", "mv_c"))
        ve_x, ve_b, ve_c = (sb(n, [P, 1]) for n in ("ve_x", "ve_b", "ve_c"))
        rs_x, rs_b, rs_c = (sb(n, [P, 1]) for n in ("rs_x", "rs_b", "rs_c"))
        ve_a, rs_a = (sb(n, [P, 2]) for n in ("ve_a", "rs_a"))
        warm = sb("warm", [P, 1])
        lg_t = sb("lg_t", [P, P])
        lg, top8, is_largest, is_second, count, taken, chosen, side = (
            sb(n, [P, NE]) for n in "lg top8 is_largest is_second count taken chosen side".split())
        gap, above, rth = (sb(n, [P, 1]) for n in ("gap", "above", "rth"))
        comb = sb("comb", [P, NE])
        comb3 = sb("comb3", [P, 3, NE], BF16)
        crest = sb("crest", [P, NE])
        comb3_t = sb("comb3_t", [P, P], BF16)
        h = sb("h", [P, EC, P])
        hs = sb("hs", [P, P])
        hc = sb("hc", [P, EC, P])

        S = es.enter_context(nc.psum_tensor("S", [P, NR, 2, 2, P], F32))
        G = [es.enter_context(nc.psum_tensor(f"G{i}", [P, 512], F32)) for i in range(4)]

        m_in, vec_in, wq_ld, wk_ld, wv_ld, wo_ld, wb_ld, wc_ld = (
            sem(n) for n in "m_in vec_in wq_ld wk_ld wv_ld wo_ld wb_ld wc_ld".split())
        x_ld = [sem(f"x_ld{i}") for i in range(2)]
        c_ld = [sem(f"c_ld{i}") for i in range(2)]
        out_st = [sem(f"out_st{i}") for i in range(2)]
        k_pool, k_fill, k_dve, k_mask, k_pe, k_ready = (
            sem(n) for n in "k_pool k_fill k_dve k_mask k_pe k_ready".split())
        (xn_ve, xn_rs, xn_ok, xbo_ok, t1_mm, t1_sb, qa_mm, ka_mm, qa_sb, ka_sb, v_mm, v_sb, sma_mm, nma_ok,
         mta_mm, mta_sb, sta_mm, ea_ok, em_ok, sa_mm, oa_mm, oa_sb, woa_mm, ya_ok, vea_ok, rsa_ok,
         xr_ok) = (sem(n) for n in (
             "xn_ve xn_rs xn_ok xbo_ok t1_mm t1_sb qa_mm ka_mm qa_sb ka_sb v_mm v_sb sma_mm nma_ok "
             "mta_mm mta_sb sta_mm ea_ok em_ok sa_mm oa_mm oa_sb woa_mm ya_ok vea_ok rsa_ok "
             "xr_ok").split())
        (col_ok, bm_ok, mk_mm, mk_sb, km_ok, qm_ok, tx_mm, tx_sb, kb_mm, kb_sb, qb_mm, qb_sb, gb_mm, gate_ok,
         smb_mm, nmb_ok, mtb_mm, mtb_sb, stb_mm, eb_ok, sb_mm, ob_mm, ob_sb, wob_mm, zb_ok, veb_ok, rsb_ok, x2_ok, x2b_ok) = (
             sem(n) for n in (
                 "col_ok bm_ok mk_mm mk_sb km_ok qm_ok tx_mm tx_sb kb_mm kb_sb qb_mm qb_sb gb_mm gate_ok "
                 "smb_mm nmb_ok mtb_mm mtb_sb stb_mm eb_ok sb_mm ob_mm ob_sb wob_mm zb_ok veb_ok rsb_ok x2_ok x2b_ok").split())
        (ty_mm, ty_sb, dn2_mm, lgt_sb, dn1_mm, lt_mm, gap_ok, rth_ok, comb_ok, ct_mm, ct_sb,
         h_ok, ce_mm, hc_ok, up_mm, yc_ok, vec_ok, rsc_ok, out_ok) = (sem(n) for n in (
             "ty_mm ty_sb dn2_mm lgt_sb dn1_mm lt_mm gap_ok rth_ok comb_ok ct_mm ct_sb "
             "h_ok ce_mm hc_ok up_mm yc_ok vec_ok rsc_ok out_ok").split())

        def wait(eng, signal, n):
            if isinstance(n, int):
                n = min(n, NB)
                if n <= 0:
                    return
            eng.wait_ge(signal, n)

        def schedule(eng, step):
            for s in (0, 1):
                step(s, s % 2)
            with eng.Fori(2, NB - 3, 2) as i:
                step(i, 0)
                step(i + 1, 1)
            for s in range(NB - 2, NB + 2):
                step(s, s % 2)

        def live(s, lag):
            return not isinstance(s, int) or 0 <= s - lag < NB

        block = es.enter_context(nc.Block())

        @block.sync
        def _(sp):
            def load_x(b, p):
                sp.dma_start(x_in[p][:, :], x[bass.ds(b, 1), :, :].rearrange("a t d -> (a t) d")).then_inc(x_ld[p], 16)

            def load_c(b, p):
                sp.dma_start(c_t[p][:, :, :], ctx_in[bass.ds(b, 1), :, :, :].rearrange("a p k t -> (a p) k t")).then_inc(c_ld[p], 16)

            load_x(0, 0)
            sp.dma_start(vecs[:, :], cols_in).then_inc(vec_in, 16)
            for i, loaded in enumerate((wq_ld, wk_ld, wv_ld)):
                sp.dma_start(wa[:, :, i, :], wa_in[:, :, i, :]).then_inc(loaded, 16)
            load_c(0, 0)
            load_x(1, 1)
            sp.dma_start(wb[:, :, :, :], wb_in).then_inc(wb_ld, 16)

            def step(s, p):
                if not isinstance(s, int) or s + 2 < NB:
                    wait(sp, xn_ok, s + 1)
                    wait(sp, xbo_ok, s + 1)
                    load_x(s + 2, p)
                if not isinstance(s, int) or s + 1 < NB:
                    wait(sp, kb_mm, s)
                    load_c(s + 1, 1 - p)
                if live(s, 2):
                    wait(sp, out_ok, s - 1)
                    sp.dma_start(out[bass.ds(s - 2, 1), :, :].rearrange("a t d -> (a t) d"),
                                 o_out[p][:, :]).then_inc(out_st[p], 16)

            schedule(sp, step)
            for p in range(2):
                sp.wait_ge(out_st[p], 16 * NB // 2)

        @block.gpsimd
        def _(pool):
            gp = nc.gpsimd
            gp.memset(identf[:, :], 0.0)
            gp.memset(identb[:, :], 0.0).then_inc(k_pool, 1)
            pool.wait_ge(k_pool, 1)
            gp.affine_select(out=identf[:, :], in_=identf[:, :], compare_op=ALU.not_equal, fill=1.0,
                             base=0, pattern=[[-1, P]], channel_multiplier=1)
            gp.affine_select(out=identb[:, :], in_=identb[:, :], compare_op=ALU.not_equal, fill=1.0,
                             base=0, pattern=[[-1, P]], channel_multiplier=1).then_inc(k_pool, 1)

            def patterns():
                gp.memset(causal[:, :], 0.0)
                gp.memset(head_row[:, :, :], 1.0)
                gp.memset(expert_row[:, :, :], 0.0).then_inc(k_pool, 1)
                pool.wait_ge(k_pool, 3)
                gp.affine_select(out=causal[:, :], in_=causal[:, :], compare_op=ALU.is_ge, fill=BIG,
                                 base=0, pattern=[[-1, P]], channel_multiplier=1)
                gp.affine_select(out=head_row[:, :, :], in_=head_row[:, :, :], compare_op=ALU.is_equal, fill=0.0,
                                 base=0, pattern=[[1, NH], [0, P]], channel_multiplier=-1)
                for part in range(3):
                    if part:
                        pool.wait_ge(k_pool, 3 + part)
                    last = gp.affine_select(out=expert_row[:, :, :].rearrange("e j (a b) -> e j a b", a=2),
                                            in_=expert_row[:, :, :].rearrange("e j (a b) -> e j a b", a=2),
                                            compare_op=ALU.not_equal, fill=0.5, base=NE * part,
                                            pattern=[[2, EC], [1, 2], [0, BD]], channel_multiplier=-1)
                    last.then_inc(k_pool, 1)

            def rstd(ve, rs, ve_ok, rs_ok, n):
                wait(pool, ve_ok, n)
                gp.tensor_tensor(rs[:, :], ve[:, :], neg_half[:, 0:rs.shape[1]], ALU.pow).then_inc(rs_ok, 1)

            def residual(n, p):
                wait(pool, ya_ok, n - 2)
                gp.tensor_tensor(x_bo[p][:, :], x_in[p][:, :], row_bc[:, 0, :], ALU.add).then_inc(xbo_ok, 1)

            def queries_b(n):
                wait(pool, qb_sb, n)
                for a in range(2):
                    last = gp.tensor_tensor(q_m[:, a, :, :], q_b[:, :, a, :],
                                            other[:, a:a + 1].unsqueeze(1).to_broadcast([P, KC, P]), ALU.add)
                last.then_inc(qm_ok, 1)

            pool.wait_ge(k_fill, 1)
            rstd(ve_x, rs_x, xn_ve, xn_rs, 1)
            patterns()

            def step(s, p):
                if live(s + 1, 0):
                    rstd(ve_x, rs_x, xn_ve, xn_rs, s + 2)
                if isinstance(s, int) and s == 0:
                    pool.wait_ge(k_ready, 1)
                    residual(1, 0)
                if live(s + 1, 0):
                    residual(s + 2, 1 - p)
                if live(s, 0):
                    wait(pool, ob_mm, s - 1)
                    gp.tensor_copy(cols[p][:, :], key_cols[:, bass.ds(s, 1), :].rearrange("p a c -> p (a c)")).then_inc(col_ok, 1)
                if live(s, 1) and not live(s, 0):
                    queries_b(s)
                if live(s, 2):
                    rstd(ve_b, rs_b, veb_ok, rsb_ok, s - 1)
                if live(s, 2) and not live(s, 1):
                    rstd(ve_c, rs_c, vec_ok, rsc_ok, s - 2)
                if live(s, 1) and live(s, 0):
                    queries_b(s)
                if live(s, 2):
                    wait(pool, x2_ok, s - 1)
                    wait(pool, yc_ok, s - 2)
                    gp.tensor_tensor(x2_b[:, :], x2[:, :], row_bc[:, 1, :], ALU.add).then_inc(x2b_ok, 1)
                if live(s, 0):
                    wait(pool, col_ok, s + 1)
                    wait(pool, ea_ok, s + 1)
                    gp.tensor_tensor(den_b[p][:, 0::2, :], den_a[:, 0::2, :],
                                     cols[p][:, 1:2].unsqueeze(1).to_broadcast([P, 2, DH]), ALU.mult).then_inc(bm_ok, 1)
                    gp.affine_select(out=e_a[:, :, :, :, :].rearrange("p r c a q -> p (r c a) q"),
                                     in_=e_a[:, :, :, :, :].rearrange("p r c a q -> p (r c a) q"),
                                     compare_op=ALU.is_ge, fill=0.0, base=0, pattern=[[0, NH], [1, P]],
                                     channel_multiplier=-1).then_inc(em_ok, 1)
                if live(s, 2) and (live(s, 0) or not live(s, 1)):
                    rstd(ve_c, rs_c, vec_ok, rsc_ok, s - 1)
                if live(s, 0):
                    rstd(ve_a, rs_a, vea_ok, rsa_ok, s + 1)

            schedule(pool, step)

        @block.scalar
        def _(act):
            ac = nc.scalar
            act.dma_start(mask_u8[:, :], mask).then_inc(m_in, 16)
            act.dma_start(rows[:, :, :], rows_in).then_inc(wo_ld, 16)
            act.dma_start(bsd_col[:, :], bsd_in).then_inc(wc_ld, 16)
            act.wait_ge(k_fill, 1)
            ac.activation(warm[:, :], neg_half[:, 0:1], ACT.Exp)
            act.wait_ge(wq_ld, 16)
            act.dma_start(wo_a[:, :, :], wo_a_in).then_inc(wo_ld, 16)
            act.dma_start(wdn[:, :, :], wdn_in).then_inc(wc_ld, 16)
            act.dma_start(wsu[:, :], wsu_in).then_inc(wc_ld, 16)
            act.dma_start(wup[:, :, :], wup_in).then_inc(wc_ld, 16)
            act.wait_ge(vec_in, 16)

            def first_t(s):
                wait(act, t1_mm, s + 1)
                for k in range(KC):
                    last = ac.activation(t1[:, k, :], G[2][:, k * P:(k + 1) * P], ACT.Identity,
                                         scale=g_col[:, k:k + 1], bias=b_col[:, k:k + 1])
                last.then_inc(t1_sb, 1)

            def keys_a(n):
                wait(act, ka_mm, n)
                for c in range(KC):
                    last = ac.activation(k_a[:, c, :], G[1][:, c * P:(c + 1) * P], ACT.Identity,
                                         bias=bk_col[:, c:c + 1])
                last.then_inc(ka_sb, 1)

            def queries_a(n):
                wait(act, qa_mm, n)
                wait(act, sta_mm, n - 1)
                for c in range(KC):
                    for a in range(2):
                        last = ac.activation(q_a[:, c, a, :], G[3][:, c * P:(c + 1) * P], ACT.Identity,
                                             scale=parity[:, a:a + 1], bias=bq_par[:, c, a:a + 1])
                last.then_inc(qa_sb, 1)

            first_t(0)
            act.wait_ge(k_mask, 1)
            queries_a(1)
            keys_a(1)

            def step(s, p):
                A, B, B2 = live(s, 0), live(s, 1), live(s, 2)

                def turned_maxima_b():
                    wait(act, mtb_mm, s)
                    ac.activation(nmt_b[0:NH, :], S[0:NH, 0, 0, 0, 0:64].bitcast(BF16), ACT.Copy).then_inc(mtb_sb, 1)

                if isinstance(s, int) and s == 1:
                    act.wait_ge(wc_ld, 64)
                if A or B:
                    act.wait_ge(v_mm, s + 1)
                if A:
                    wait(act, oa_mm, s)
                    last = ac.activation(v_a[:, :, 0::2, :], G[0][:, 0:256].rearrange("p (a b d) -> p a b d", b=2, d=DH), ACT.Copy)
                if B:
                    wait(act, bm_ok, s)
                    wait(act, ob_mm, s - 2)
                    last = ac.activation(v_b[1 - p][:, :, 0::2, :], G[0][:, 256:512].rearrange("p (a b d) -> p a b d", b=2, d=DH),
                                         ACT.Copy, scale=cols[1 - p][:, 0:1])
                if A or B:
                    last.then_inc(v_sb, 1)
                if B:
                    wait(act, tx_mm, s)
                    wait(act, gb_mm, s - 1)
                    for k in range(KC):
                        last = ac.activation(t2[:, 0, k, :], G[2][:, k * P:(k + 1) * P], ACT.Copy,
                                             scale=nw_col[:, k:k + 1])
                    last.then_inc(tx_sb, 1)
                    wait(act, kb_mm, s)
                    ac.activation(k_b[:, :, :].rearrange("p c t -> p (c t)"), G[0][:, 0:256], ACT.Copy).then_inc(kb_sb, 1)
                if A:
                    wait(act, mta_mm, s + 1)
                    ac.activation(nmt_a[0:NH, :], S[0:NH, 0, 0, 0, 0:64].bitcast(BF16), ACT.Copy).then_inc(mta_sb, 1)
                if live(s + 1, 0):
                    first_t(s + 1)
                if B:
                    wait(act, qb_mm, s)
                    for a in range(2):
                        last = ac.activation(q_b[:, :, a, :], G[3][:, 0:256].rearrange("p (c t) -> p c t", c=KC),
                                             ACT.Copy, scale=parity[:, a:a + 1])
                    last.then_inc(qb_sb, 1)
                if A:
                    wait(act, mk_mm, s + 1)
                    wait(act, km_ok, s - 1)
                    for a in range(2):
                        last = ac.activation(mask_t[p][:, a, :], G[2][:, 256:256 + P], ACT.Copy, scale=other[:, a:a + 1])
                    last.then_inc(mk_sb, 1)
                if B2:
                    wait(act, ty_mm, s - 1)
                    ac.activation(t2[:, 1, :, :].rearrange("p k t -> p (k t)"), G[1][:, 0:256], ACT.Copy).then_inc(ty_sb, 1)
                if B:
                    wait(act, gb_mm, s)
                    wait(act, zb_ok, s - 1)
                    ac.activation(gate[:, :], G[3][:, 0:256], ACT.Tanh, scale=0.5).then_inc(gate_ok, 1)
                if B2:
                    wait(act, dn2_mm, s - 1)
                    ac.activation(lg_t[BD:BD + NE, :], G[1][BD:BD + NE, 0:P], ACT.Copy).then_inc(lgt_sb, 1)
                    ac.activation(hs[0:BD, :], G[1][0:BD, 0:P], ACT.Gelu, bias=bsd_col[:, :])
                    wait(act, gap_ok, s - 1)
                    ac.activation(rth[:, :], gap[:, :], ACT.Tanh, scale=0.5).then_inc(rth_ok, 1)
                    if B and not A:
                        turned_maxima_b()
                    wait(act, dn1_mm, s - 1)
                    for j in range(EC):
                        last = ac.activation(h[:, j, :], G[0][:, j * P:(j + 1) * P], ACT.Gelu, bias=bd_col[:, j:j + 1])
                    last.then_inc(h_ok, 1)
                    ac.activation(warm[:, :], neg_half[:, 0:1], ACT.Exp)
                if A:
                    wait(act, sta_mm, s + 1)
                    ac.activation(e_a[:, :, :, :, :].rearrange("p r c a q -> p (r c a q)"),
                                  S[:, :, :, :, :].rearrange("p r c a q -> p (r c a q)"), ACT.Exp,
                                  scale=SCALE).then_inc(ea_ok, 1)
                if live(s + 1, 0):
                    keys_a(s + 2)
                    queries_a(s + 2)
                if B and A:
                    turned_maxima_b()
                if B:
                    wait(act, stb_mm, s)
                    ac.activation(e_b[:, :, :, :, :].rearrange("p r c a q -> p (r c a q)"),
                                  S[:, :, :, :, :].rearrange("p r c a q -> p (r c a q)"), ACT.Exp,
                                  scale=SCALE, bias=cols[1 - p][:, 2:3]).then_inc(eb_ok, 1)

            schedule(act, step)

        @block.vector
        def _(dve):
            v = nc.vector

            def set_up():
                for k in range(KC):
                    v.tensor_scalar(bq_par[:, k, :], parity[:, :], bq_col[:, k:k + 1], None, ALU.mult)
                    v.tensor_scalar(bvb[:, k, :], ones[:, :], bv_col[:, k:k + 1], None, ALU.mult)
                dve.wait_ge(m_in, 16)
                v.tensor_copy(mask_f[:, :], mask_u8[:, :]).then_inc(k_dve, 1)
                dve.drain()
                v.reduce_max(mask_any[:, 0:1], mask_f[:, :], axis=AX.X)
                dve.drain()
                v.tensor_scalar(mask_any[:, 1:2], mask_any[:, 0:1], -1.0, 1.0, ALU.mult, ALU.add)
                dve.drain()
                v.tensor_scalar(mask_g[:, :], mask_f[:, :], mask_any[:, 1:2], None, ALU.max)
                dve.drain()
                v.tensor_scalar(mask_add[0:NB, :], mask_g[:, :], -BIG, BIG, ALU.mult, ALU.add).then_inc(k_mask, 1)
                dve.wait_ge(k_pe, 1)
                v.tensor_copy(valid[:, :], G[0][:, 0:NB]).then_inc(k_dve, 1)
                dve.drain()
                v.tensor_copy(key_cols[:, :, 0], valid[:, :])

            def set_up_rows():
                dve.wait_ge(k_pe, 2)
                v.tensor_scalar(none_valid[:, :], G[1][:, 0:NB], 0.5, None, ALU.is_lt)
                dve.drain()
                v.tensor_tensor(key_cols[:, :, 1], none_valid[:, :], valid[:, :], ALU.max)
                dve.drain()
                v.tensor_scalar(key_cols[:, :, 2], key_cols[:, :, 1], -BIG, BIG, ALU.mult, ALU.add)
                v.tensor_copy(row_bc[:, :, :].rearrange("p a n -> p (a n)"), G[3][:, :]).then_inc(k_ready, 1)

            def stats(y, st, mv, ve, ve_ok, rms=False):
                v.bn_stats(st[:, :], y)
                dve.drain()
                v.bn_aggr(mv[:, :], st[:, :])
                dve.drain()
                last = v.tensor_scalar(ve[:, 0:1], mv[:, 1:2], EPS_LN, None, ALU.add)
                if rms:
                    last = v.tensor_scalar(ve[:, 1:2], mv[:, 1:2], 1.0 + EPS_RMS, EPS_RMS * EPS_LN, ALU.mult, ALU.add)
                last.then_inc(ve_ok, 1)

            def first_norm(n, p, loaded):
                dve.wait_ge(x_ld[p], loaded)
                stats(x_in[p][:, :], st_x, mv_x, ve_x, xn_ve)
                wait(dve, xn_rs, n)
                if not isinstance(n, int) or n > 1:
                    dve.wait_ge(t1_mm, n - 1)
                v.tensor_scalar(xn[:, :], x_in[p][:, :], mv_x[:, 0:1], rs_x[:, :], ALU.subtract, ALU.mult).then_inc(xn_ok, 1)

            for tile, value in ((neg_half, -0.5), (ones, 1.0), (mask_add, 0.0),
                                (comb3_t, 0.0), (hs, 0.0), (nmt_a, 0.0), (nmt_b, 0.0)):
                v.memset(tile[:, :], value)
            for tile, value in ((v_a, 0.0), (v_b[0], 0.0), (v_b[1], 0.0)):
                v.memset(tile[:, :, :, :], value)
            for tile, value in ((den_a, 1.0), (den_b[0], 0.0), (den_b[1], 0.0)):
                v.memset(tile[:, :, :], value)
            dve.drain()
            v.memset(den_a[:, 1:2, :], 0.0).then_inc(k_fill, 1)
            dve.wait_ge(k_pool, 2)
            v.reduce_sum(parity[:, :], identf[:, :].rearrange("p (r a d) -> p a r d", a=2, d=DH), axis=AX.XY)
            first_norm(1, 0, 16)
            v.tensor_scalar(other[:, :], parity[:, :], -1.0, 1.0, ALU.mult, ALU.add)
            dve.wait_ge(vec_in, 16)
            set_up()

            def router(n):
                wait(dve, lt_mm, n)
                v.tensor_copy(lg[:, :], G[2][:, 0:NE])
                dve.drain()
                v.max(top8[:, :], lg[:, :])
                largest, second = top8[:, 0:1], top8[:, 1:2]
                dve.drain()
                v.tensor_tensor(gap[:, :], largest, second, ALU.subtract).then_inc(gap_ok, 1)
                v.tensor_scalar(is_second[:, :], lg[:, :], second, None, ALU.is_equal)
                v.tensor_tensor(above[:, :], largest, second, ALU.is_gt)
                v.tensor_scalar(is_largest[:, :], lg[:, :], largest, 2.0, ALU.is_equal, ALU.mult)
                dve.drain()
                v.tensor_tensor_scan(count[:, :], ones[:, 0:NE], is_second[:, :], above[:, :], ALU.mult, ALU.add)
                dve.drain()
                v.scalar_tensor_tensor(out=taken[:, :], in0=count[:, :], scalar=2.0, in1=is_second[:, :],
                                       op0=ALU.is_le, op1=ALU.mult)
                dve.drain()
                v.scalar_tensor_tensor(out=chosen[:, :], in0=lg[:, :], scalar=second, in1=taken[:, :],
                                       op0=ALU.is_gt, op1=ALU.add)
                dve.drain()
                v.scalar_tensor_tensor(out=side[:, :], in0=is_largest[:, :], scalar=1.0, in1=chosen[:, :],
                                       op0=ALU.subtract, op1=ALU.mult)
                dve.drain()
                wait(dve, rth_ok, n)
                for dst in (comb[:, :], comb3[:, 0, :]):
                    v.scalar_tensor_tensor(out=dst, in0=side[:, :], scalar=rth[:, :], in1=chosen[:, :],
                                           op0=ALU.mult, op1=ALU.add)
                dve.drain()
                v.tensor_tensor(crest[:, :], comb[:, :], comb3[:, 0, :], ALU.subtract)
                dve.drain()
                v.tensor_copy(comb3[:, 1, :], crest[:, :])
                dve.drain()
                v.tensor_tensor(comb3[:, 2, :], crest[:, :], comb3[:, 1, :], ALU.subtract).then_inc(comb_ok, 1)

            def step(s, p):
                A, B, B2 = live(s, 0), live(s, 1), live(s, 2)

                def add_c(n):
                    wait(dve, up_mm, n)
                    wait(dve, x2b_ok, n)
                    v.tensor_tensor(y_c[:, :], G[2][:, 0:256], x2_b[:, :], ALU.add).then_inc(yc_ok, 1)
                    dve.drain()
                    stats(y_c[:, :], st_c, mv_c, ve_c, vec_ok)

                def norm_c(n, p):
                    wait(dve, rsc_ok, n)
                    if not isinstance(n, int) or n >= 3:
                        dve.wait_ge(out_st[p], 8 * n - 8 - 8 * p)
                    v.tensor_scalar(o_out[p][:, :], y_c[:, :], mv_c[:, 0:1], rs_c[:, :], ALU.subtract, ALU.mult).then_inc(out_ok, 1)

                def keys_b():
                    wait(dve, kb_sb, s)
                    wait(dve, mk_sb, s)
                    for a in range(2):
                        last = v.scalar_tensor_tensor(out=k_m[:, a, :, :], in0=k_b[:, :, :], scalar=parity[:, a:a + 1],
                                                      in1=mask_t[1 - p][:, a, :].unsqueeze(1).to_broadcast([P, KC, P]),
                                                      op0=ALU.mult, op1=ALU.add)
                    last.then_inc(km_ok, 1)

                def maxima_b():
                    wait(dve, smb_mm, s)
                    v.tensor_reduce(nm_b[:, :], S[:, :, :, :, :].rearrange("p r c a k -> p (r c a) k"),
                                    op=ALU.max, axis=AX.X, negate=True).then_inc(nmb_ok, 1)

                if live(s + 1, 0):
                    first_norm(s + 2, 1 - p, 8 * (s + 1) + 16 - 8 * (1 - p))
                if B2:
                    wait(dve, sb_mm, s - 1)
                    v.reciprocal(rec_b[:, :], G[1][:, 0:256])
                    dve.drain()
                    wait(dve, ob_mm, s - 1)
                    v.tensor_tensor(o_b[:, :, :].rearrange("p c t -> p (c t)"), G[3][:, 0:256], rec_b[:, :], ALU.mult).then_inc(ob_sb, 1)
                if A:
                    wait(dve, sma_mm, s + 1)
                    v.tensor_reduce(nm_a[:, :], S[:, :, :, :, :].rearrange("p r c a k -> p (r c a) k"),
                                    op=ALU.max, axis=AX.X, negate=True).then_inc(nma_ok, 1)
                if isinstance(s, int) and s == 0:
                    set_up_rows()
                if B2:
                    wait(dve, wob_mm, s - 1)
                    v.scalar_tensor_tensor(out=z_b[:, :], in0=gate[:, :], scalar=1.0, in1=G[1][:, 0:256],
                                           op0=ALU.add, op1=ALU.mult).then_inc(zb_ok, 1)
                    if B and not A:
                        keys_b()
                    dve.drain()
                    v.scalar_tensor_tensor(out=y_b[:, :], in0=z_b[:, :], scalar=0.5, in1=x1[p][:, :],
                                           op0=ALU.mult, op1=ALU.add)
                    dve.drain()
                    stats(y_b[:, :], st_b, mv_b, ve_b, veb_ok)
                    wait(dve, rsb_ok, s - 1)
                    wait(dve, x2b_ok, s - 2)
                    v.tensor_scalar(x2[:, :], y_b[:, :], mv_b[:, 0:1], rs_b[:, :], ALU.subtract, ALU.mult).then_inc(x2_ok, 1)
                if B2 and not B:
                    add_c(s - 2)
                    norm_c(s - 2, 1 - p)
                if B and A:
                    keys_b()
                if B and not A:
                    maxima_b()
                if B2:
                    router(s - 1)
                    wait(dve, ct_mm, s - 1)
                    v.tensor_copy(comb3_t[0:3 * NE, :], G[2][0:3 * NE, 0:64].bitcast(BF16))
                    v.tensor_scalar(hs[BD:BD + NE, :], G[2][0:NE, 64:192], 0.5, None, ALU.mult).then_inc(ct_sb, 1)
                    wait(dve, ce_mm, s - 1)
                    wait(dve, h_ok, s - 1)
                    v.tensor_tensor(hc[:, :, :].rearrange("p j t -> p (j t)"), h[:, :, :].rearrange("p j t -> p (j t)"),
                                    G[0][:, :], ALU.mult).then_inc(hc_ok, 1)
                if A and B:
                    maxima_b()
                if A:
                    wait(dve, sa_mm, s + 1)
                    v.reciprocal(rec_a[:, :], G[0][:, 0:256])
                    dve.drain()
                    wait(dve, oa_mm, s + 1)
                    v.tensor_tensor(o_a[:, :, :].rearrange("p c t -> p (c t)"), G[3][:, 0:256], rec_a[:, :], ALU.mult).then_inc(oa_sb, 1)
                if B2 and (A or not B):
                    add_c(s - 1)
                    norm_c(s - 1, p)
                if A:
                    wait(dve, woa_mm, s + 1)
                    wait(dve, xbo_ok, s + 1)
                    v.tensor_tensor(y_a[:, :], G[1][:, 0:256], x_bo[p][:, :], ALU.add).then_inc(ya_ok, 1)
                    dve.drain()
                    stats(y_a[:, :], st_a, mv_a, ve_a, vea_ok, rms=True)
                    wait(dve, rsa_ok, s + 1)
                    v.tensor_scalar(xr[:, :], y_a[:, :], mv_a[:, 0:1], rs_a[:, 1:2], ALU.subtract, ALU.mult).then_inc(xr_ok, 1)
                    v.tensor_scalar(x1[p][:, :], y_a[:, :], mv_a[:, 0:1], rs_a[:, 0:1], ALU.subtract, ALU.mult)

            schedule(dve, step)

        @block.tensor
        def _(pe):
            mm = nc.tensor.matmul

            def project_t(dst, w, i, src):
                for m in range(KC):
                    for k in range(KC):
                        last = mm(dst[:, m * P:(m + 1) * P], w[:, k, i, m * P:(m + 1) * P], src[:, k, :],
                                  start=(k == 0), stop=(k == KC - 1))
                return last

            def project(dst, src, w, i):
                for k in range(KC):
                    last = mm(dst, src[:, k, :], w[:, k, i, :], start=(k == 0), stop=(k == KC - 1))
                return last

            def high(t):
                return t.bitcast(BF16)

            def products(pairs, start):
                for c, a, q, k in pairs:
                    for r in range(NR):
                        g = slice(32 * r, 32 * r + 32)
                        last = mm(S[:, r, c, a, :], q[g, :], k[g, :], start=(start and c == 0 and a == 0),
                                  stop=True, skip_group_check=True)
                return last

            def scores_for_max_a():
                for r in range(NR):
                    mm(S[:, r, :, :, :].rearrange("p c a k -> p (c a) k"), identb[:, :],
                       causal[:, :].unsqueeze(1).to_broadcast([P, 4, P]), start=True, stop=False, skip_group_check=True)
                return products([(c, a, high(q_a[:, c, a, :])[:, 1::2], high(k_a[:, c, :])[:, 1::2])
                                 for c in range(KC) for a in range(2)], False)

            def scores_t(q, k, nmt, c):
                for r in range(NR):
                    for a in range(2):
                        mm(S[:, r, c, a, :], head_row[:, 4 * r + 2 * c + a, :], nmt[:, :],
                           start=(c == 0 and a == 0), stop=False, skip_group_check=True)
                for r in range(NR):
                    g = slice(32 * r, 32 * r + 32)
                    last = mm(S[:, r, c, :, :], k[g, c, :], q[g, c, :, :], start=False, stop=True,
                              skip_group_check=True)
                return last

            def values(dst, v_, e):
                for c in range(KC):
                    for a in range(2):
                        for r in range(NR):
                            last = mm(dst[32 * r:32 * r + 32, c * P:(c + 1) * P],
                                      v_[:, 4 * c + r, a:a + 2, :].rearrange("p a d -> p (a d)"), e[:, r, c, a, :],
                                      start=(a == 0), stop=(a == 1))
                return last

            def sums(dst, e, den):
                for a in range(2):
                    for r in range(NR):
                        last = mm(dst[32 * r:32 * r + 32, 0:256].rearrange("p (c q) -> p c q", c=KC),
                                  den[:, a:a + 2, :].rearrange("p a d -> p (a d)"), e[:, r, :, a, :],
                                  start=(a == 0), stop=(a == 1))
                return last

            def turn(dst, src):
                for k in range(KC):
                    last = nc.tensor.transpose(dst[:, k * P:(k + 1) * P], src[:, k * P:(k + 1) * P], identf[:, :])
                return last

            def first_t(s):
                wait(pe, xn_ok, s + 1)
                turn(G[2][:, 0:256], xn).then_inc(t1_mm, 1)

            def query_a(s):
                pe.wait_ge(t1_sb, s + 1)
                project_t(G[3][:, 0:256], wa, 0, t1).then_inc(qa_mm, 1)

            def key_a(s):
                project_t(G[1][:, 0:256], wa, 1, t1).then_inc(ka_mm, 1)

            def keep_clock(dst, n):
                for _ in range(n):
                    mm(dst[:, 0:P], ones[:, :], ones[:, :], start=True, stop=True)

            pe.wait_ge(k_pool, 2)
            first_t(0)
            pe.wait_ge(k_dve, 1)
            nc.tensor.transpose(G[0][:, 0:NB], mask_f[:, :], identf[0:NB, 0:NB]).then_inc(k_pe, 1)
            pe.wait_ge(wq_ld, 16)
            query_a(0)
            pe.wait_ge(wk_ld, 16)
            key_a(0)

            def set_up_rows():
                pe.wait_ge(k_dve, 2)
                pe.wait_ge(ka_sb, 1)
                mm(G[1][:, 0:NB], ones[:, :], valid[:, :], start=True, stop=True)
                pe.wait_ge(wo_ld, 32)
                mm(G[3][:, 0:D], ones[0:1, :], rows[:, 0, :], start=True, stop=False)
                for k in range(KC):
                    mm(G[3][:, 0:D], bvb[:, k, :], wo_a[:, k, :], start=False, stop=(k == KC - 1))
                mm(G[3][:, D:2 * D], ones[0:1, :], rows[:, 1, :], start=True, stop=True).then_inc(k_pe, 1)

            def step(s, p):
                A, B, B2 = live(s, 0), live(s, 1), live(s, 2)
                if isinstance(s, int) and s == 0:
                    pe.wait_ge(wv_ld, 16)
                    pe.wait_ge(k_dve, 2)
                    pe.wait_ge(k_pool, 6)
                if isinstance(s, int) and s == 1:
                    pe.wait_ge(wb_ld, 16)
                    pe.wait_ge(wc_ld, 64)

                def gate_b():
                    wait(pe, qb_sb, s)
                    project(G[3][:, 0:256], t2[:, 0, :, :], wb, 1).then_inc(gb_mm, 1)

                def maxima_b():
                    wait(pe, qm_ok, s)
                    wait(pe, km_ok, s)
                    wait(pe, ea_ok, s + 1)
                    products([(c, a, q_m[:, a, c, :], k_m[:, a, c, :]) for c in range(KC) for a in range(2)],
                             True).then_inc(smb_mm, 1)

                def up(n, part):
                    if part == 0:
                        wait(pe, ct_sb, n)
                        mm(G[2][:, 0:256], hs[:, :], wsu[:, :], start=True, stop=False)
                        return
                    wait(pe, hc_ok, n)
                    for j in range(EC):
                        last = mm(G[2][:, 0:256], hc[:, j, :], wup[:, j, :], start=False, stop=(j == EC - 1))
                    last.then_inc(up_mm, 1)

                def turn_maxima_b():
                    wait(pe, nmb_ok, s)
                    nc.tensor.transpose(S[0:NH, 0, 0, 0, 0:64].bitcast(BF16), nm_b[:, :], identb[:, :]).then_inc(mtb_mm, 1)

                if A:
                    wait(pe, t1_sb, s + 1)
                if A or B:
                    wait(pe, oa_sb, s)
                if A:
                    last = project(G[0][:, 0:256], t1, wa, 2)
                if B:
                    pe.wait_ge(c_ld[1 - p], 8 * (s - 1) + 16 - 8 * (1 - p))
                    last = project(G[0][:, 256:512], c_t[1 - p], wb, 3)
                if A or B:
                    last.then_inc(v_mm, 1)
                if A and not B2:
                    wait(pe, qa_sb, s + 1)
                    wait(pe, ka_sb, s + 1)
                    wait(pe, ea_ok, s)
                    scores_for_max_a().then_inc(sma_mm, 1)
                if isinstance(s, int) and s == 0:
                    set_up_rows()
                if B:
                    wait(pe, yc_ok, s - 2)
                    wait(pe, xr_ok, s)
                    turn(G[2][:, 0:256], xr).then_inc(tx_mm, 1)
                if B2:
                    wait(pe, eb_ok, s - 1)
                    wait(pe, ya_ok, s)
                    sums(G[1], e_b, den_b[p]).then_inc(sb_mm, 1)
                    wait(pe, oa_sb, s)
                    values(G[3], v_b[p], e_b).then_inc(ob_mm, 1)
                if A and B2:
                    wait(pe, qa_sb, s + 1)
                    wait(pe, ka_sb, s + 1)
                    wait(pe, eb_ok, s - 1)
                    scores_for_max_a().then_inc(sma_mm, 1)
                if B:
                    pe.wait_ge(v_sb, s + 1)
                    project_t(G[0][:, 0:256], wb, 2, c_t[1 - p]).then_inc(kb_mm, 1)
                if B2:
                    wait(pe, ob_sb, s - 1)
                    project(G[1][:, 0:256], o_b, wb, 4).then_inc(wob_mm, 1)
                if B2 and not B:
                    up(s - 2, 1)
                if B:
                    wait(pe, tx_sb, s)
                    wait(pe, ob_sb, s - 1)
                    wait(pe, oa_sb, s)
                    project_t(G[3][:, 0:256], wb, 0, t2[:, 0, :, :]).then_inc(qb_mm, 1)
                if A:
                    wait(pe, nma_ok, s + 1)
                    nc.tensor.transpose(S[0:NH, 0, 0, 0, 0:64].bitcast(BF16), nm_a[:, :], identb[:, :]).then_inc(mta_mm, 1)
                wait(pe, tx_sb, s)
                if A:
                    if isinstance(s, int) and s == 0:
                        pe.wait_ge(k_mask, 1)
                    mm(G[2][:, 256:256 + P], head_row[:, bass.ds(s, 1), :].rearrange("p a t -> p (a t)"), mask_add[:, :],
                       start=True, stop=True).then_inc(mk_mm, 1)
                if live(s + 1, 0):
                    first_t(s + 1)
                if A:
                    wait(pe, mta_sb, s + 1)
                    scores_t(q_a, k_a, nmt_a, 0)
                if B and not A:
                    gate_b()
                    maxima_b()
                if B2:
                    wait(pe, x2_ok, s - 1)
                    wait(pe, zb_ok, s - 1)
                    turn(G[1][:, 0:256], x2).then_inc(ty_mm, 1)
                if B and A:
                    gate_b()
                if B2:
                    wait(pe, ty_sb, s - 1)
                    for k in range(KC):
                        last = mm(G[1][0:BD + NE, 0:P], wdn[:, k, NE * BD:], t2[:, 1, k, :], start=(k == 0), stop=(k == KC - 1))
                    last.then_inc(dn2_mm, 1)
                    wait(pe, kb_sb, s)
                    for j in range(EC):
                        if j == (2 if A else 1):
                            wait(pe, lgt_sb, s - 1)
                            wait(pe, t1_sb, s + 2)
                            wait(pe, mk_sb, s + 1)
                            wait(pe, yc_ok, s - 2)
                            wait(pe, tx_sb, s)
                            mm(G[2][:, 0:NE], lg_t[BD:BD + NE, :], identf[BD:BD + NE, BD:BD + NE],
                               start=True, stop=True).then_inc(lt_mm, 1)
                        for k in range(KC):
                            last = mm(G[0][:, j * P:(j + 1) * P], wdn[:, k, j * P:(j + 1) * P], t2[:, 1, k, :],
                                      start=(k == 0), stop=(k == KC - 1))
                    last.then_inc(dn1_mm, 1)
                if A:
                    scores_t(q_a, k_a, nmt_a, 1).then_inc(sta_mm, 1)
                if live(s + 1, 0):
                    wait(pe, gate_ok, s)
                    if isinstance(s, int) and s == 0:
                        pe.wait_ge(k_ready, 1)
                    query_a(s + 1)
                if B and not A:
                    turn_maxima_b()
                    wait(pe, mtb_sb, s)
                    scores_t(q_b, k_b, nmt_b, 0)
                if B2:
                    if not B:
                        keep_clock(G[3], 6)
                    wait(pe, comb_ok, s - 1)
                    nc.tensor.transpose(G[2][0:NE, 64:192], comb[:, :], identf[:, :])
                    nc.tensor.transpose(G[2][0:3 * NE, 0:64].bitcast(BF16), comb3[:, :, :].rearrange("p a e -> p (a e)"),
                                        identb[:, :]).then_inc(ct_mm, 1)
                if B and not A:
                    scores_t(q_b, k_b, nmt_b, 1).then_inc(stb_mm, 1)
                if live(s + 1, 0):
                    wait(pe, h_ok, s - 1)
                    key_a(s + 1)
                if B2:
                    wait(pe, ct_sb, s - 1)
                    wait(pe, h_ok, s - 1)
                    for j in range(EC):
                        last = mm(G[0][:, j * P:(j + 1) * P], expert_row[:, j, :], comb3_t[:, :], start=True, stop=True)
                    last.then_inc(ce_mm, 1)
                if B2:
                    up(s - 1, 0)
                    if B and not A:
                        keep_clock(G[1], 5)
                if A and B:
                    maxima_b()
                if B2 and (A or not B):
                    up(s - 1, 1)
                if A:
                    wait(pe, em_ok, s + 1)
                    wait(pe, hc_ok, s - 1)
                    wait(pe, v_sb, s + 1)
                    wait(pe, kb_sb, s)
                    sums(G[0], e_a, den_a).then_inc(sa_mm, 1)
                if A and B:
                    turn_maxima_b()
                if A:
                    wait(pe, qa_sb, s + 2)
                    wait(pe, gate_ok, s)
                    values(G[3], v_a, e_a).then_inc(oa_mm, 1)
                if A and B:
                    wait(pe, mtb_sb, s)
                    scores_t(q_b, k_b, nmt_b, 0)
                if A:
                    wait(pe, oa_sb, s + 1)
                    wait(pe, ka_sb, s + 2)
                    for k in range(KC):
                        last = mm(G[1][:, 0:256], o_a[:, k, :], wo_a[:, k, :], start=(k == 0), stop=(k == KC - 1))
                    last.then_inc(woa_mm, 1)
                if A and B:
                    scores_t(q_b, k_b, nmt_b, 1).then_inc(stb_mm, 1)

            schedule(pe, step)


_OUT = ((NB, P, D), "float32")


def kernel(x, ctx_2048, mask_BxS2_bk0, L0_attn_ln_g, L0_attn_ln_b, L0_attn_Wq, L0_attn_bq, L0_attn_Wk,
           L0_attn_bk, L0_attn_Wv, L0_attn_bv, L0_attn_Wo, L0_attn_bo, L0_xattn_norm_w, L0_xattn_wq,
           L0_xattn_wk, L0_xattn_wv, L0_xattn_wo, L0_xattn_wg, L0_ffn_gate_w, L0_ffn_wd, L0_ffn_bd,
           L0_ffn_wu, L0_ffn_bu, L0_ffn_ws_d, L0_ffn_bs_d, L0_ffn_ws_u, L0_ffn_bs_u):
    import numpy as np
    import concourse.bacc as bacc
    from concourse.bass_utils import run_bass_kernel_spmd

    A = np.asarray

    def k_rows(*ws):
        w = np.concatenate(ws, axis=1)
        return w.reshape(-1, P, w.shape[1]).transpose(1, 0, 2)

    def columns(*vs):
        return np.concatenate([A(v).reshape(-1, P) for v in vs]).T

    wd, wu = A(L0_ffn_wd), A(L0_ffn_wu)
    laid_out = [
        ("x", A(x)), ("ctx", A(ctx_2048).reshape(NB, P, KC, P).transpose(0, 3, 2, 1)), ("mask", A(mask_BxS2_bk0)),
        ("vectors", columns(L0_attn_ln_g, L0_attn_ln_b, L0_xattn_norm_w, L0_attn_bq, L0_attn_bk, L0_attn_bv,
                            L0_ffn_bd)),
        ("rows", np.stack([A(L0_attn_bo), A(L0_ffn_bs_u)])[None]),
        ("wa", k_rows(A(L0_attn_Wq), A(L0_attn_Wk), A(L0_attn_Wv)).reshape(P, KC, 3, D)),
        ("wo_a", k_rows(A(L0_attn_Wo))),
        ("wb", k_rows(A(L0_xattn_wq).T, A(L0_xattn_wg).T, A(L0_xattn_wk).T, A(L0_xattn_wv).T,
                      A(L0_xattn_wo).T).reshape(P, KC, 5, D)),
        ("wdn", k_rows(wd.reshape(-1, D).T, A(L0_ffn_ws_d).T, A(L0_ffn_gate_w).T)),
        ("wup", k_rows(wu.transpose(0, 2, 1).reshape(-1, D))),
        ("wsu", np.concatenate([A(L0_ffn_ws_u).T, A(L0_ffn_bu), np.zeros((P - BD - NE, D), np.float32)])),
        ("bsd", A(L0_ffn_bs_d)[:, None]),
    ]
    nc = bacc.Bacc("TRN2", target_bir_lowering=False, num_devices=1)
    arrays, args = {}, []
    for name, a in laid_out:
        a = np.ascontiguousarray(a)
        arrays[f"in_{name}"] = a
        args.append(nc.dram_tensor(f"in_{name}", a.shape, mybir.dt.from_np(a.dtype), kind="ExternalInput").ap())
    out = nc.dram_tensor("out", _OUT[0], mybir.dt.from_np(np.dtype(_OUT[1])), kind="ExternalOutput").ap()
    decoder_layer(nc, *args, out)
    r = run_bass_kernel_spmd(nc, [arrays], core_ids=[0])
    return r.results[0]["out"]
```
